# Optimizing a Trainium2 kernel written in Bass

```python
import numpy as np
import jax
import jax.numpy as jnp

def _softmax(x, axis=-1):
    return jax.nn.softmax(x, axis=axis)

def _gelu(x):
    return jax.nn.gelu(x, approximate=True)

def _silu(x):
    return jax.nn.silu(x)

def _sigmoid(x):
    return jax.nn.sigmoid(x)

def _layernorm(x, axis=-1, eps=1e-05):
    m = jnp.mean(x, axis=axis, keepdims=True)
    v = jnp.var(x, axis=axis, keepdims=True)
    return (x - m) / jnp.sqrt(v + eps)

def _scatter_add(tgt, idx, src, axis=0):
    return tgt.at[idx].add(src)

def _segment_sum(src, seg, n):
    return jax.ops.segment_sum(src, seg, n)
kernel_name = 'mk_vit_tower_d2_tok_img256_r4_a0c09e'

def setup_inputs(seed: int=0):
    np.random.seed(seed)
    _w = jnp.asarray

    def _rec_inputs():
        import jax
        import jax.numpy as jnp
        _rk = jax.random.key(seed)
        x = -4.65018e-05 + 0.999886 * jax.random.normal(jax.random.fold_in(_rk, 1), (8, 3, 128, 128), jnp.float32)
        return x
    x = _rec_inputs()

    def _L0_tok_setup():
        import jax, jax.numpy as jnp
        import numpy as np
        B, C, H, P, D = (64, 3, 128, 16, 64)
        NP = H // P
        key = jax.random.key(seed)
        ks = jax.random.split(key, 7)
        s = lambda fan_in: 1.0 / np.sqrt(fan_in)
        return {'x': jax.random.normal(ks[0], (B, C, H, H), dtype=jnp.float32), 'Wp': jax.random.normal(ks[1], (P * P * C, D), dtype=jnp.float32) * s(P * P * C), 'bp': jax.random.normal(ks[2], (D,), dtype=jnp.float32) * 0.01, 'W1': jax.random.normal(ks[3], (2, D), dtype=jnp.float32) * s(2), 'b1': jax.random.normal(ks[4], (D,), dtype=jnp.float32) * 0.01, 'W2': jax.random.normal(ks[5], (D, D), dtype=jnp.float32) * s(D), 'b2': jax.random.normal(ks[6], (D,), dtype=jnp.float32) * 0.01}
    _L0_tok_all = _L0_tok_setup()
    _L0_tok_in = {k: v for k, v in _L0_tok_all.items() if k in ('Wp', 'bp', 'W1', 'b1', 'W2', 'b2')}
    del _L0_tok_all

    def _L0_attn_setup():
        import jax, jax.numpy as jnp
        import numpy as np
        B, S, C = (8, 256, 64)
        H, KD = (8, 64)
        HEAD_DIM = KD // H
        key = jax.random.key(seed)
        ks = jax.random.split(key, 5)
        sc = 0.02
        return {'x': jax.random.normal(ks[0], (B, S, C), dtype=jnp.float32), 'Wq': jax.random.normal(ks[1], (H * KD, C), dtype=jnp.float32) * sc, 'Wk': jax.random.normal(ks[2], (KD, C), dtype=jnp.float32) * sc, 'Wv': jax.random.normal(ks[3], (KD, C), dtype=jnp.float32) * sc, 'Wo': jax.random.normal(ks[4], (C, H * KD), dtype=jnp.float32) * sc}
    _L0_attn_all = _L0_attn_setup()
    _L0_attn_in = {k: v for k, v in _L0_attn_all.items() if k in ('Wq', 'Wk', 'Wv', 'Wo')}
    del _L0_attn_all

    def _L0_ffn_setup():
        import jax, jax.numpy as jnp
        import numpy as np
        B, S, D = (8, 1024, 64)
        H = 4 * D
        CAPACITY = 0.5
        key = jax.random.key(seed)
        ks = jax.random.split(key, 6)
        x = jax.random.normal(ks[0], (B, S, D), dtype=jnp.float32)
        attention_mask = jnp.zeros((B, 1, 1, S), dtype=jnp.float32)
        wr = jax.random.normal(ks[1], (D, 1), dtype=jnp.float32) * 0.02
        br = jnp.zeros((1,), dtype=jnp.float32)
        w1 = jax.random.normal(ks[2], (D, H), dtype=jnp.float32) * 0.02
        b1 = jnp.zeros((H,), dtype=jnp.float32)
        w2 = jax.random.normal(ks[3], (H, D), dtype=jnp.float32) * 0.02
        b2 = jnp.zeros((D,), dtype=jnp.float32)
        return {'x': x, 'attention_mask': attention_mask, 'wr': wr, 'br': br, 'w1': w1, 'b1': b1, 'w2': w2, 'b2': b2}
    _L0_ffn_all = _L0_ffn_setup()
    _L0_ffn_in = {k: v for k, v in _L0_ffn_all.items() if k in ('attention_mask', 'wr', 'br', 'w1', 'b1', 'w2', 'b2')}
    del _L0_ffn_all

    def _L1_attn_setup():
        import jax, jax.numpy as jnp
        import numpy as np
        H = 8
        key = jax.random.key(seed)
        ks = jax.random.split(key, 10)
        B, N, D, E = (1, 1024, 64, 16384)
        s = 0.02
        return {'x': jax.random.normal(ks[0], (B, N, D), jnp.float32), 'edge_index': jax.random.randint(ks[1], (2, E), 0, N, jnp.int32), 'edge_attr': jax.random.normal(ks[2], (E, 3), jnp.float32), 'Wq': jax.random.normal(ks[3], (D, D), jnp.float32) * s, 'bq': jnp.zeros((D,), jnp.float32), 'Wk': jax.random.normal(ks[4], (D, D), jnp.float32) * s, 'bk': jnp.zeros((D,), jnp.float32), 'Wv': jax.random.normal(ks[5], (D, D), jnp.float32) * s, 'bv': jnp.zeros((D,), jnp.float32), 'Wo': jax.random.normal(ks[6], (D, D), jnp.float32) * s, 'bo': jnp.zeros((D,), jnp.float32), 'We': jax.random.normal(ks[7], (3, H), jnp.float32) * s, 'be': jnp.zeros((H,), jnp.float32)}
    _L1_attn_all = _L1_attn_setup()
    _L1_attn_in = {k: v for k, v in _L1_attn_all.items() if k in ('edge_index', 'edge_attr', 'Wq', 'bq', 'Wk', 'bk', 'Wv', 'bv', 'Wo', 'bo', 'We', 'be')}
    del _L1_attn_all

    def _L1_ffn_setup():
        import jax, jax.numpy as jnp
        import numpy as np
        NUM_EXPERTS = 8
        TOP_K = 2
        B, S, D = (8, 2048, 64)

        def _moe(tokens, router_w, w1, b1, w2, b2):
            N = tokens.shape[0]
            E = router_w.shape[0]
            logits = tokens.astype(jnp.float32) @ router_w.astype(jnp.float32).T
            probs = jax.nn.softmax(logits, axis=-1)
            rw, re = jax.lax.top_k(probs, TOP_K)
            if TOP_K > 1:
                rw = rw / jnp.maximum(rw.sum(-1, keepdims=True), 1e-12)
            rw = rw.astype(tokens.dtype)
            combine = jnp.zeros((N, E), tokens.dtype).at[jnp.arange(N)[:, None], re].set(rw)
            out = tokens
            for e in range(E):
                h = jax.nn.gelu(tokens @ w1[e] + b1[e], approximate=False)
                y = h @ w2[e] + b2[e]
                out = out + combine[:, e:e + 1] * y
            return out
        key = jax.random.key(seed)
        ks = jax.random.split(key, 4)
        scale = 1.0 / np.sqrt(D).astype(np.float32)
        return {'input_embeddings': jax.random.normal(ks[0], (B, S, D), jnp.float32), 'router_w': jax.random.normal(ks[1], (NUM_EXPERTS, D), jnp.float32) * scale, 'w1': jax.random.normal(ks[2], (NUM_EXPERTS, D, D), jnp.float32) * scale, 'b1': jnp.zeros((NUM_EXPERTS, D), jnp.float32), 'w2': jax.random.normal(ks[3], (NUM_EXPERTS, D, D), jnp.float32) * scale, 'b2': jnp.zeros((NUM_EXPERTS, D), jnp.float32)}
    _L1_ffn_all = _L1_ffn_setup()
    _L1_ffn_in = {k: v for k, v in _L1_ffn_all.items() if k in ('router_w', 'w1', 'b1', 'w2', 'b2')}
    del _L1_ffn_all
    return {'x': x, 'L0_tok_Wp': _L0_tok_in['Wp'], 'L0_tok_bp': _L0_tok_in['bp'], 'L0_tok_W1': _L0_tok_in['W1'], 'L0_tok_b1': _L0_tok_in['b1'], 'L0_tok_W2': _L0_tok_in['W2'], 'L0_tok_b2': _L0_tok_in['b2'], 'L0_attn_Wq': _L0_attn_in['Wq'], 'L0_attn_Wk': _L0_attn_in['Wk'], 'L0_attn_Wv': _L0_attn_in['Wv'], 'L0_attn_Wo': _L0_attn_in['Wo'], 'L0_ffn_attention_mask': _L0_ffn_in['attention_mask'], 'L0_ffn_wr': _L0_ffn_in['wr'], 'L0_ffn_br': _L0_ffn_in['br'], 'L0_ffn_w1': _L0_ffn_in['w1'], 'L0_ffn_b1': _L0_ffn_in['b1'], 'L0_ffn_w2': _L0_ffn_in['w2'], 'L0_ffn_b2': _L0_ffn_in['b2'], 'L1_attn_edge_index': _L1_attn_in['edge_index'], 'L1_attn_edge_attr': _L1_attn_in['edge_attr'], 'L1_attn_Wq': _L1_attn_in['Wq'], 'L1_attn_bq': _L1_attn_in['bq'], 'L1_attn_Wk': _L1_attn_in['Wk'], 'L1_attn_bk': _L1_attn_in['bk'], 'L1_attn_Wv': _L1_attn_in['Wv'], 'L1_attn_bv': _L1_attn_in['bv'], 'L1_attn_Wo': _L1_attn_in['Wo'], 'L1_attn_bo': _L1_attn_in['bo'], 'L1_attn_We': _L1_attn_in['We'], 'L1_attn_be': _L1_attn_in['be'], 'L1_ffn_router_w': _L1_ffn_in['router_w'], 'L1_ffn_w1': _L1_ffn_in['w1'], 'L1_ffn_b1': _L1_ffn_in['b1'], 'L1_ffn_w2': _L1_ffn_in['w2'], 'L1_ffn_b2': _L1_ffn_in['b2']}

def reference(x, L0_tok_Wp, L0_tok_bp, L0_tok_W1, L0_tok_b1, L0_tok_W2, L0_tok_b2, L0_attn_Wq, L0_attn_Wk, L0_attn_Wv, L0_attn_Wo, L0_ffn_attention_mask, L0_ffn_wr, L0_ffn_br, L0_ffn_w1, L0_ffn_b1, L0_ffn_w2, L0_ffn_b2, L1_attn_edge_index, L1_attn_edge_attr, L1_attn_Wq, L1_attn_bq, L1_attn_Wk, L1_attn_bk, L1_attn_Wv, L1_attn_bv, L1_attn_Wo, L1_attn_bo, L1_attn_We, L1_attn_be, L1_ffn_router_w, L1_ffn_w1, L1_ffn_b1, L1_ffn_w2, L1_ffn_b2):
    import jax
    import jax.numpy as jnp

    def _L0_tok_ref(x, Wp, bp, W1, b1, W2, b2):
        import jax, jax.numpy as jnp
        import numpy as np
        B, C, H, P, D = (64, 3, 128, 16, 64)
        NP = H // P
        b = x.shape[0]
        patches = x.reshape(b, C, NP, P, NP, P)
        patches = patches.transpose(0, 2, 4, 1, 3, 5).reshape(b, NP * NP, C * P * P)
        embedded = jnp.einsum('bnk,kd->bnd', patches, Wp) + bp
        gx, gy = jnp.meshgrid(jnp.arange(NP, dtype=jnp.float32), jnp.arange(NP, dtype=jnp.float32), indexing='ij')
        xy = jnp.stack([gx, gy], axis=-1).reshape(1, -1, 2) / (NP - 1)
        pos = jax.nn.relu(xy @ W1 + b1) @ W2 + b2
        return embedded + pos

    def _L0_attn_ref(x, Wq, Wk, Wv, Wo):
        import jax, jax.numpy as jnp
        import numpy as np
        B, S, C = (8, 256, 64)
        H, KD = (8, 64)
        HEAD_DIM = KD // H
        b, s, c = x.shape
        q = jnp.einsum('bsc,oc->bso', x, Wq).reshape(b, s, H, KD).transpose(0, 2, 1, 3)
        k = jnp.einsum('bsc,oc->bos', x, Wk)
        v_conv = jnp.einsum('bsc,oc->bos', x, Wv)
        v = v_conv.reshape(b, s, KD)
        scale = 1.0 / np.sqrt(HEAD_DIM).astype(np.float32)
        scores = jnp.einsum('bhsd,bdt->bhst', q, k) * scale
        attn = jax.nn.softmax(scores, axis=-1)
        ctx = jnp.einsum('bhst,btd->bhsd', attn, v)
        ctx = ctx.transpose(0, 2, 1, 3).reshape(b, H * KD, s)
        out = jnp.einsum('bcp,oc->bop', ctx, Wo)
        return out.transpose(0, 2, 1)

    def _L0_ffn_ref(x, attention_mask, wr, br, w1, b1, w2, b2):
        import jax, jax.numpy as jnp
        import numpy as np
        B, S, D = (8, 1024, 64)
        H = 4 * D
        CAPACITY = 0.5
        b, s, d = x.shape
        weights = (jnp.einsum('bsd,do->bso', x, wr) + br)[..., 0]
        k = max(1, int(CAPACITY * s))
        kk = k - 1 if k > 1 else 1
        _, idx = jax.lax.top_k(weights, k)
        sel_idx = idx[:, :kk]
        sel = jnp.take_along_axis(x, sel_idx[:, :, None], axis=1)
        h = jax.nn.gelu(jnp.einsum('bkd,dh->bkh', sel, w1) + b1)
        y = jnp.einsum('bkh,hd->bkd', h, w2) + b2
        w_sel = jnp.take_along_axis(weights, sel_idx, axis=1)
        y = y * w_sel[..., None]
        batch_idx = jnp.arange(b)[:, None]
        processed = jnp.zeros_like(x).at[batch_idx, sel_idx].set(y)
        return processed + x

    def _L1_attn_ref(x, edge_index, edge_attr, Wq, bq, Wk, bk, Wv, bv, Wo, bo, We, be):
        import jax, jax.numpy as jnp
        import numpy as np
        H = 8
        B, N, D = x.shape
        hd = D // H
        q = (x @ Wq + bq).reshape(B, N, H, hd)
        k = (x @ Wk + bk).reshape(B, N, H, hd)
        v = (x @ Wv + bv).reshape(B, N, H, hd)
        scores = jnp.einsum('bihd,bjhd->bhij', q, k) / jnp.sqrt(jnp.asarray(hd, x.dtype))
        eb = edge_attr @ We + be
        edge_tgt = edge_index[1]
        col_bias = jnp.zeros((H, N), x.dtype).at[:, edge_tgt].set(eb.T)
        scores = scores + col_bias[None, :, None, :]
        attn = jax.nn.softmax(scores, axis=-1)
        out = jnp.einsum('bhij,bjhd->bihd', attn, v).reshape(B, N, D)
        return out @ Wo + bo

    def _L1_ffn_ref(input_embeddings, router_w, w1, b1, w2, b2):
        import jax, jax.numpy as jnp
        import numpy as np
        NUM_EXPERTS = 8
        TOP_K = 2
        B, S, D = (8, 2048, 64)

        def _moe(tokens, router_w, w1, b1, w2, b2):
            N = tokens.shape[0]
            E = router_w.shape[0]
            logits = tokens.astype(jnp.float32) @ router_w.astype(jnp.float32).T
            probs = jax.nn.softmax(logits, axis=-1)
            rw, re = jax.lax.top_k(probs, TOP_K)
            if TOP_K > 1:
                rw = rw / jnp.maximum(rw.sum(-1, keepdims=True), 1e-12)
            rw = rw.astype(tokens.dtype)
            combine = jnp.zeros((N, E), tokens.dtype).at[jnp.arange(N)[:, None], re].set(rw)
            out = tokens
            for e in range(E):
                h = jax.nn.gelu(tokens @ w1[e] + b1[e], approximate=False)
                y = h @ w2[e] + b2[e]
                out = out + combine[:, e:e + 1] * y
            return out
        b, s, d = input_embeddings.shape
        tokens = input_embeddings.reshape(b * s, d)
        return _moe(tokens, router_w, w1, b1, w2, b2).reshape(b, s, d)
    h = _L0_tok_ref(x, L0_tok_Wp, L0_tok_bp, L0_tok_W1, L0_tok_b1, L0_tok_W2, L0_tok_b2)
    h = h + _L0_attn_ref(_layernorm(h, axis=-1), L0_attn_Wq, L0_attn_Wk, L0_attn_Wv, L0_attn_Wo)
    h = h + _L0_ffn_ref(_layernorm(h, axis=-1), L0_ffn_attention_mask, L0_ffn_wr, L0_ffn_br, L0_ffn_w1, L0_ffn_b1, L0_ffn_w2, L0_ffn_b2)
    h = h + _L1_attn_ref(_layernorm(h, axis=-1), L1_attn_edge_index, L1_attn_edge_attr, L1_attn_Wq, L1_attn_bq, L1_attn_Wk, L1_attn_bk, L1_attn_Wv, L1_attn_bv, L1_attn_Wo, L1_attn_bo, L1_attn_We, L1_attn_be)
    h = h + _L1_ffn_ref(_layernorm(h, axis=-1), L1_ffn_router_w, L1_ffn_w1, L1_ffn_b1, L1_ffn_w2, L1_ffn_b2)
    return h

_drawn_inputs = setup_inputs


def setup_inputs(seed=0):
    import zlib

    import numpy as np

    out = dict(_drawn_inputs(seed))
    spreads = {'L0_ffn_b1': (0.0, 0.8),
     'L0_ffn_b2': (0.0, 0.8),
     'L1_attn_bq': (0.0, 0.8),
     'L1_attn_bk': (0.0, 2.0),
     'L1_attn_bv': (0.0, 0.8),
     'L1_attn_bo': (0.0, 0.327),
     'L1_attn_be': (0.0, 2.0),
     'L1_ffn_b1': (0.0, 0.494),
     'L1_ffn_b2': (0.0, 0.324)}
    factors = {'L0_tok_bp': 5.232,
     'L0_tok_b1': 5.907,
     'L0_tok_b2': 3.975,
     'L0_attn_Wq': 8.0,
     'L0_attn_Wk': 8.0,
     'L0_attn_Wv': 4.805,
     'L0_attn_Wo': 4.999,
     'L0_ffn_wr': 8.0,
     'L0_ffn_w1': 8.0,
     'L0_ffn_w2': 8.0,
     'L1_attn_edge_attr': 8.0,
     'L1_attn_Wq': 8.0,
     'L1_attn_Wk': 8.0,
     'L1_attn_Wv': 8.0,
     'L1_attn_Wo': 4.63,
     'L1_attn_We': 8.0}
    for name, (base, spread) in spreads.items():
        noise = np.random.default_rng([zlib.crc32(name.encode()), seed]).standard_normal(out[name].shape)
        drawn = base * np.exp(spread * noise) if base else spread * noise
        out[name] = jnp.asarray(drawn.astype(out[name].dtype))
    for name, factor in factors.items():
        out[name] = (out[name] * factor).astype(out[name].dtype)
    return out
```

```python
import numpy as np
import concourse.bass as bass
from concourse import mybir
from contextlib import ExitStack


def vit_tower(nc, I, grid, out):
    fp32 = mybir.dt.float32
    bf16 = mybir.dt.bfloat16
    i32 = mybir.dt.int32
    u32 = mybir.dt.uint32
    ALU = mybir.AluOpType
    ACT = mybir.ActivationFunctionType
    X = mybir.AxisListType.X

    BATCH, CH, SIDE, _ = I["x"].shape
    D = I["L0_tok_Wp"].shape[1]
    PATCH = 16
    NP = SIDE // PATCH
    TOK = NP * NP
    NT = BATCH * TOK
    P = 128
    SLOTS = NT // P
    HALF = NT // 2
    HEADS = 8
    HD = D // HEADS
    KROWS = CH * PATCH
    EDGES = I["L1_attn_edge_index"].shape[1]
    ROWE = EDGES // P
    EXPERTS = I["L1_ffn_w1"].shape[0]
    HID = I["L0_ffn_w1"].shape[1]
    KSEL = max(1, TOK // 2) - 1
    SC0 = 1.0 / float(np.sqrt(np.float32(8)))
    SC0_INV = float(np.nextafter(np.float32(1) / np.float32(SC0), np.float32(4)))
    EPS = 1e-5
    EXPO = 127
    ABSENT = D * EXPO

    ctx = ExitStack()
    with ctx:
        def sb(name, shape, dt=fp32):
            return ctx.enter_context(nc.sbuf_tensor(name, shape, dt))

        def sem(name):
            return ctx.enter_context(nc.semaphore(name))

        ident = sb("ident", [P, P])
        eye2 = sb("eye2", [P, TOK])
        earlier = sb("earlier", [P, TOK])
        earlier8 = sb("earlier8", [P, EXPERTS, EXPERTS])
        ones_row = sb("ones_row", [1, P])
        neg_half = sb("neg_half", [P, SLOTS])
        euler = sb("euler", [P, SLOTS * EXPERTS])
        zeros_row = sb("zeros_row", [P, 8])
        iota16 = sb("iota16", [P, 16, P], bf16)
        row_bits = sb("row_bits", [P, 2], i32)
        row_pow = sb("row_pow", [P, 2], bf16)
        col_idx = sb("col_idx", [P, 1])
        Xt = sb("Xt", [2 * KROWS, BATCH // 2, NP, SIDE])
        Wbd = sb("Wbd", [P, PATCH, 2, D])
        gridT = sb("gridT", [3, TOK])
        posW1 = sb("posW1", [3, D])
        posW2 = sb("posW2", [D, 2, D])
        rows = sb("rows", [8, P])
        cols = sb("cols", [P, 8])
        qk_rows = sb("qk_rows", [4, P])
        qk_cols = sb("qk_cols", [P, 4])
        Wq0 = sb("Wq0", [P, 4, D])
        Wk0 = sb("Wk0", [P, D])
        Wv0 = sb("Wv0", [D, D])
        Wo0 = sb("Wo0", [D, TOK * HEADS])
        wvT = sb("wvT", [D, 2, D])
        WoR = sb("WoR", [D, 4, 2, TOK])
        WoT = sb("WoT", [P, 4, D])
        G = sb("G", [D, HEADS, D])
        wr = sb("wr", [D, 1])
        br = sb("br", [P, 1])
        w1f = sb("w1f", [D, HID])
        w2f = sb("w2f", [P, HID // P, D])
        b2f = sb("b2f", [1, D])
        ids = sb("ids", [P, ROWE], i32)
        Wq1 = sb("Wq1", [D, D])
        Wk1 = sb("Wk1", [D, D])
        Wv1 = sb("Wv1", [D, D])
        Wo1 = sb("Wo1", [D, D])
        WqP = sb("WqP", [D, 2, P])
        WkP = sb("WkP", [D, 2, P])
        bv_rep = sb("bv_rep", [P, D])
        bo_rep = sb("bo_rep", [P, D])
        WeB = sb("WeB", [4, HEADS])
        rw = sb("rw", [EXPERTS, D])
        rwT = sb("rwT", [D, EXPERTS])
        w1e = sb("w1e", [D, EXPERTS, D])
        w2e = sb("w2e", [P, EXPERTS // 2, D])
        b2e = sb("b2e", [EXPERTS, D])

        idf = sb("idf", [P, 3, ROWE])
        idb = sb("idb", [P, 4, ROWE], bf16)
        onehot = sb("onehot", [P, TOK, ROWE], bf16)
        expo = sb("expo", [P, TOK, 2], i32)
        last = sb("last", [P, 3, TOK])
        edge = sb("edge", [TOK, 4])
        edge_u = sb("edge_u", [TOK, 1], u32)
        attr = sb("attr", [TOK, 4])
        attrT = sb("attrT", [4, TOK])
        biasP = sb("biasP", [TOK, 2, P])
        kbias = sb("kbias", [P, 2, TOK])

        posh = sb("posh", [D, TOK])
        pos = sb("pos", [P, TOK])
        embT = sb("embT", [P, 2, P])
        h = [sb(f"h{i}", [P, SLOTS, D]) for i in range(5)]
        stats = sb("stats", [P, 4, SLOTS, 6])
        mv = sb("mv", [P, 4, SLOTS, 2])
        var = sb("var", [P, 4, SLOTS])
        rstd = sb("rstd", [P, 4, SLOTS])
        xn = [sb(f"xn{i}", [P, SLOTS, 2, D]) for i in range(4)]
        xT = [sb(f"xT{i}", [P, NT]) for i in range(4)]
        res = [sb(f"res{i}", [P, SLOTS, D]) for i in range(4)]
        qT0 = sb("qT0", [P, 2, BATCH, 2, TOK])
        v0 = sb("v0", [P, NT])
        top0 = sb("top0", [P, 3, SLOTS, HEADS])
        E0 = sb("E0", [P, SLOTS, HEADS, TOK])
        WoS = sb("WoS", [P, SLOTS, HEADS, D])
        M0 = sb("M0", [P, SLOTS, D])
        hid = sb("hid", [P, 2, NT])
        wall = sb("wall", [P, SLOTS, TOK])
        wdiag = sb("wdiag", [P, SLOTS, TOK])
        wcol = sb("wcol", [P, SLOTS])
        tie = sb("tie", [P, SLOTS, TOK])
        ahead = sb("ahead", [P, SLOTS, TOK])
        rank = sb("rank", [P, SLOTS])
        gate = sb("gate", [P, SLOTS])
        qT1 = sb("qT1", [P, 2, NT])
        kT1 = sb("kT1", [P, 2, NT])
        vB = sb("vB", [P, BATCH, 4, 2 * (HD + 1)])
        top1 = sb("top1", [P, SLOTS, HEADS])
        E1 = sb("E1", [P, SLOTS, HEADS, TOK])
        ET = sb("ET", [P, SLOTS, 4, P])
        rden = sb("rden", [P, SLOTS, HEADS])
        ctxn = sb("ctxn", [P, SLOTS, D])
        ctxT = sb("ctxT", [D, NT])
        lg = sb("lg", [P, SLOTS, EXPERTS])
        lgm = sb("lgm", [P, SLOTS])
        lgd = sb("lgd", [P, SLOTS, EXPERTS])
        lge = sb("lge", [P, SLOTS, EXPERTS])
        better = sb("better", [P, 3, SLOTS * EXPERTS, EXPERTS])
        erank = sb("erank", [P, SLOTS * EXPERTS])
        esel = sb("esel", [P, SLOTS, EXPERTS])
        esum = sb("esum", [P, 2, SLOTS])
        comb = sb("comb", [P, SLOTS, EXPERTS])
        combT = sb("combT", [EXPERTS, NT])
        part = sb("part", [P, 2, SLOTS, EXPERTS])
        comb3 = sb("comb3", [P, SLOTS, 3, EXPERTS], bf16)
        comb3T = sb("comb3T", [3 * EXPERTS, NT], bf16)
        sel3 = sb("sel3", [3 * EXPERTS, 4, P], bf16)
        ident_h = sb("ident_h", [P, P], bf16)
        ge = sb("ge", [P, 4, NT])
        gs = sb("gs", [P, 4, NT])

        psum = ctx.enter_context(nc.psum_tensor("psum", [P, 8, 512], fp32))
        B = [psum[:, i, :] for i in range(8)]

        in_ids, in_wp, in_pos = sem("in_ids"), sem("in_wp"), sem("in_pos")
        in_x = [sem("in_x0"), sem("in_x1")]
        in_l0, in_f0, in_l1, in_moe = sem("in_l0"), sem("in_f0"), sem("in_l1"), sem("in_moe")
        in_rows, in_attr, out_done = sem("in_rows"), sem("in_attr"), sem("out_done")
        wbd_zero, const_step, const_id = sem("wbd_zero"), sem("const_step"), sem("const_id")
        const_edge, const_l1, const_sel = sem("const_edge"), sem("const_l1"), sem("const_sel")
        rows_zero, rows_one = sem("rows_zero"), sem("rows_one")
        padded = sem("padded")
        s_wor = sem("wo_regrouped")
        s_posh, s_posh_ev, s_pos, s_cols_ev = sem("posh_ps"), sem("posh_ready"), sem("pos_ps"), sem("cols_ready")
        s_pos_ev = sem("pos_ready")
        s_wt, s_wt_ev, s_g, s_g_ev = sem("wt_ps"), sem("wt_ready"), sem("g_ps"), sem("g_ready")
        s_hot, s_expo, s_key, s_keyT = sem("onehot_ready"), sem("expo_ps"), sem("key_ready"), sem("keyT_ps")
        s_edge, s_attrT, s_attrT_ev = sem("edge_ready"), sem("attrT_ps"), sem("attrT_ready")
        s_eb, s_biasP, s_kb, s_kb_ev = sem("edgebias_ps"), sem("biasP_ready"), sem("kbias_ps"), sem("kbias_ready")
        s_emb, s_embT, s_nat, s_h0 = sem("emb_ps"), sem("embT_ready"), sem("nat_ps"), sem("h0_ready")
        s_h = sem("h_ready")
        s_st, s_mv, s_var, s_rstd = sem("stats_done"), sem("meanvar_done"), sem("var_ready"), sem("rstd_ready")
        s_xn, s_xt, s_xt_ev, s_res = sem("xn_ready"), sem("xT_ps"), sem("xT_ready"), sem("res_ready")
        s_q0, s_q0_ev, s_v0, s_v0_ev = sem("q0_ps"), sem("q0_ready"), sem("v0_ps"), sem("v0_ready")
        s_sc0, s_mx0, s_sub0, s_exp0 = sem("scores0_ps"), sem("max0_done"), sem("shifted0"), sem("exp0_done")
        s_sum0, s_rinv, s_wos, s_wosd = sem("sum0_done"), sem("rinv_ready"), sem("wos_ready"), sem("wos3_ready")
        s_m0, s_m0_ev, s_o0 = sem("mix0_ps"), sem("mix0_ready"), sem("attn0_ps")
        s_wr, s_hid, s_gelu, s_y, s_gate = sem("weights_ps"), sem("hid_ps"), sem("gelu_ready"), sem("ffn_ps"), sem("gate_ready")
        s_vec = sem("vector_step")
        s_q1, s_q1_ev, s_k1, s_k1_ev = sem("q1_ps"), sem("q1_ready"), sem("k1_ps"), sem("k1_ready")
        s_v1, s_v1_ev, s_h2b = sem("v1_ps"), sem("v1_ready"), sem("h2_bias_ready")
        s_sc1, s_mx1, s_sub1, s_exp1 = sem("scores1_ps"), sem("max1_done"), sem("shifted1"), sem("exp1_done")
        s_et, s_et_ev_a, s_et_ev_v, s_av = sem("ET_ps"), sem("ET_ready_act"), sem("ET_ready_dve"), sem("ctx_ps")
        s_ctx, s_ctxT, s_ctxT_ev, s_o1 = sem("ctx_ready"), sem("ctxT_ps"), sem("ctxT_ready"), sem("attn1_ps")
        s_lg, s_lgd, s_lge, s_comb = sem("logits_ps"), sem("logits_shifted"), sem("logit_exp"), sem("comb_ready")
        s_eh, s_eg, s_cr, s_gs = sem("expert_hid_ps"), sem("expert_gelu"), sem("comb_rep_ps"), sem("expert_scaled")
        s_ct, s_ct_ev, s_fin, s_out_v, s_out_a = sem("combT_ps"), sem("combT_ready"), sem("moe_ps"), sem("out_dve"), sem("out_act")

        s_c3, s_c3_ev, const_moe = sem("comb3T_ps"), sem("comb3T_ready"), sem("const_moe")
        C3 = B[3][0:3 * EXPERTS, 0:NT // 2].bitcast(bf16)

        block = ctx.enter_context(nc.Block())

        def bc(ap, axis, n):
            u = ap.unsqueeze(axis)
            shape = list(u.shape)
            shape[axis] = n
            return u.broadcast_to(shape)

        x_v = I["x"].rearrange("b c (py ph) w -> c ph b py w", ph=PATCH)
        wp_v = I["L0_tok_Wp"].rearrange("(r w) d -> r w d", w=PATCH)

        def load_x(eng, g, c):
            for k in range(CH):
                r0 = g * KROWS + k * PATCH
                for b in (2 * c, 2 * c + 1):
                    eng.dma_start(Xt[r0:r0 + PATCH, b, :, :], x_v[k, :, g * 4 + b, :, :]).then_inc(in_x[c], 16)

        @block.sync
        def _(sp):
            def load(dst, src, s):
                sp.dma_start(dst, src).then_inc(s, 16)

            load(ids[:, :], I["L1_attn_edge_index"][1, :].rearrange("(p e) -> p e", p=P), in_ids)
            load_x(sp, 0, 0)
            sp.wait_ge(wbd_zero, 2)
            load(Wbd[0:KROWS, :, 0, :], wp_v, in_wp)
            load(gridT[:, :], grid, in_pos)
            load(posW1[0:2, :], I["L0_tok_W1"], in_pos)
            load(posW1[2:3, :], I["L0_tok_b1"].rearrange("(a d) -> a d", a=1), in_pos)
            load(posW2[:, :, :], bc(I["L0_tok_W2"], 1, 2), in_pos)
            load_x(sp, 0, 1)
            load(Wq0[:, :, :], I["L0_attn_Wq"].rearrange("(k p) c -> p k c", p=P), in_l0)
            load(Wk0[0:D, :], I["L0_attn_Wk"], in_l0)
            load(Wk0[D:P, :], I["L0_attn_Wk"], in_l0)
            load(Wv0[:, :], I["L0_attn_Wv"], in_l0)
            load(Wo0[:, :], I["L0_attn_Wo"], in_l0)
            load(wr[:, :], I["L0_ffn_wr"], in_f0)
            load(br[:, :], I["L0_ffn_br"].rearrange("(a d) -> a d", a=1).broadcast_to([P, 1]), in_f0)
            load(w1f[:, :], I["L0_ffn_w1"], in_f0)
            load(w2f[:, :, :], I["L0_ffn_w2"].rearrange("(k p) d -> p k d", p=P), in_f0)
            load(b2f[:, :], I["L0_ffn_b2"].rearrange("(a d) -> a d", a=1), in_f0)
            load(Wq1[:, :], I["L1_attn_Wq"], in_l1)
            load(Wk1[:, :], I["L1_attn_Wk"], in_l1)
            load(Wv1[:, :], I["L1_attn_Wv"], in_l1)
            load(Wo1[:, :], I["L1_attn_Wo"], in_l1)
            load(bv_rep[:, :], I["L1_attn_bv"].rearrange("(a d) -> a d", a=1).broadcast_to([P, D]), in_l1)
            load(bo_rep[:, :], I["L1_attn_bo"].rearrange("(a d) -> a d", a=1).broadcast_to([P, D]), in_l1)
            load(WeB[0:3, :], I["L1_attn_We"], in_l1)
            load(WeB[3:4, :], I["L1_attn_be"].rearrange("(a d) -> a d", a=1), in_l1)
            load(w1e[:, :, :], I["L1_ffn_w1"].rearrange("e d f -> d e f"), in_moe)
            load(w2e[:, :, :], I["L1_ffn_w2"].rearrange("(q e) f d -> (e f) q d", e=2), in_moe)
            load(b2e[:, :], I["L1_ffn_b2"], in_moe)
            out_v = out.rearrange("(g c b) t d -> c (b t) g d", g=2, c=2)
            sp.wait_ge(s_out_v, 1)
            sp.dma_start(out_v[0], h[4][:, 0:2, :]).then_inc(out_done, 16)
            sp.wait_ge(s_out_a, 1)
            sp.dma_start(out_v[1], h[4][:, 2:4, :]).then_inc(out_done, 16)
            sp.wait_ge(out_done, 32)

        N_L0, N_F0, N_L1, N_MOE, N_POS, N_ROWS = 5 * 16, 5 * 16, 8 * 16, 3 * 16, 4 * 16, 7 * 16

        @block.gpsimd
        def _(pool):
            gp = nc.gpsimd
            gp.memset(Wbd[:, 0:PATCH // 2, :, :], 0.0).then_inc(wbd_zero, 1)
            gp.iota(iota16[:, :, :], [[1, 16], [0, P]], base=0, channel_multiplier=0,
                    allow_small_or_imprecise_dtypes=True).then_inc(const_edge, 1)
            gp.memset(row_bits[:, :], 0).then_inc(const_step, 1)
            pool.wait_ge(const_step, 1)
            for u in range(2):
                gp.iota(row_bits[64 * u:64 * u + 64, u:u + 1], [[0, 1]], base=EXPO << 23,
                        channel_multiplier=2 << 23).then_inc(const_step, 1)
                pool.wait_ge(const_step, u + 2)
            gp.memset(ident[:, :], 0.0).then_inc(const_step, 1)
            gp.memset(rows[:, :], 0.0).then_inc(rows_zero, 1)
            gp.memset(qk_rows[:, :], 0.0).then_inc(rows_zero, 1)
            pool.wait_ge(const_step, 4)
            gp.tensor_copy(row_pow[:, :], row_bits[:, :].bitcast(fp32)).then_inc(const_edge, 1)
            gp.affine_select(out=ident[:, :], in_=ident[:, :], compare_op=ALU.not_equal, fill=1.0, base=0,
                             pattern=[[-1, P]], channel_multiplier=1).then_inc(const_id, 1)
            pool.wait_ge(rows_zero, 2)
            gp.memset(qk_rows[0:2, :].rearrange("g (h k) -> g h k", h=4)[:, :, HD:HD + 1], SC0_INV).then_inc(rows_one, 1)
            pool.wait_ge(rows_one, 1)

            def load(dst, src, s):
                pool.dma_start(dst, src).then_inc(s, 16)

            load(rows[0:1, :].rearrange("a (u d) -> a u d", u=2),
                 bc(I["L0_tok_bp"].rearrange("(a d) -> a d", a=1), 1, 2), in_rows)
            load(rows[1:2, :].rearrange("a (u d) -> a u d", u=2),
                 bc(I["L0_tok_b2"].rearrange("(a d) -> a d", a=1), 1, 2), in_rows)
            load(rows[2:4, :], I["L0_ffn_b1"].rearrange("(a d) -> a d", d=P), in_rows)
            load(rows[4:8, :], I["L1_ffn_b1"].rearrange("(q e) f -> q (e f)", e=2), in_rows)
            for n, name in enumerate(("L1_attn_bq", "L1_attn_bk")):
                load(qk_rows[2 * n:2 * n + 2, :].rearrange("g (h k) -> g h k", h=4)[:, :, 0:HD],
                     I[name].rearrange("(g h k) -> g h k", g=2, h=4), in_rows)
            load(rw[:, :], I["L1_ffn_router_w"], in_rows)
            gp.iota(col_idx[:, :], [[0, 1]], base=0, channel_multiplier=1,
                    allow_small_or_imprecise_dtypes=True).then_inc(const_edge, 1)
            gp.memset(neg_half[:, :], -0.5).then_inc(const_edge, 1)
            gp.memset(ones_row[:, :], 1.0).then_inc(const_sel, 1)
            gp.memset(euler[:, :], float(np.e)).then_inc(const_sel, 1)
            gp.memset(earlier[:, :], 1.0).then_inc(const_step, 1)
            gp.memset(earlier8[:, :, :], 1.0).then_inc(const_step, 1)
            gp.memset(eye2[:, :], 0.0).then_inc(const_step, 1)
            pool.wait_ge(const_step, 7)
            for u in range(2):
                part = slice(u * TOK, (u + 1) * TOK)
                gp.affine_select(out=eye2[part, :], in_=eye2[part, :], compare_op=ALU.not_equal, fill=1.0, base=0,
                                 pattern=[[-1, TOK]], channel_multiplier=1).then_inc(const_sel, 1)
                pool.wait_ge(const_sel, 3 + 2 * u)
                gp.affine_select(out=earlier[part, :], in_=earlier[part, :], compare_op=ALU.is_gt, fill=0.0, base=0,
                                 pattern=[[-1, TOK]], channel_multiplier=1).then_inc(const_sel, 1)
                pool.wait_ge(const_sel, 4 + 2 * u)
            gp.affine_select(out=earlier8[:, :, :], in_=earlier8[:, :, :], compare_op=ALU.is_gt, fill=0.0, base=0,
                             pattern=[[1, EXPERTS], [-1, EXPERTS]], channel_multiplier=0).then_inc(const_sel, 1)
            pool.wait_ge(const_id, 1)
            gp.tensor_copy(ident_h[:, :], ident[:, :]).then_inc(const_moe, 1)
            gp.memset(sel3[:, :, :], 0.0).then_inc(const_moe, 1)
            for n in range(3):
                pool.wait_ge(const_moe, n + 2)
                sel = sel3[:, :, :].rearrange("k q (e f) -> k (q e) f", e=2)
                gp.affine_select(out=sel, in_=sel, compare_op=ALU.not_equal, fill=1.0, base=-EXPERTS * n,
                                 pattern=[[-1, EXPERTS], [0, D]], channel_multiplier=1).then_inc(const_moe, 1)
            gp.memset(WqP[:, :, :], 0.0).then_inc(const_l1, 1)
            gp.memset(WkP[:, :, :], 0.0).then_inc(const_l1, 1)
            gp.memset(biasP[:, :, :], 0.0).then_inc(const_l1, 1)
            gp.memset(attr[:, :], 1.0).then_inc(const_l1, 1)
            gp.memset(vB[:, :, :, :], 0.0).then_inc(const_l1, 1)
            pool.wait_ge(const_l1, 5)
            for u in range(2):
                gp.memset(vB[u * TOK:(u + 1) * TOK, :, :, u * (HD + 1) + HD:u * (HD + 1) + HD + 1], 1.0).then_inc(const_l1, 1)
                pool.wait_ge(const_l1, 6 + u)

            def power(k, c):
                n = 2 * k + c
                pool.wait_ge(s_var, n + 1)
                gp.tensor_tensor(rstd[:, k, 2 * c:2 * c + 2], var[:, k, 2 * c:2 * c + 2], neg_half[:, 0:2],
                                 ALU.pow).then_inc(s_rstd, 1)

            def residual(k, c):
                n = 2 * k + c
                pool.wait_ge(s_xn, n + 1)
                sl = slice(2 * c, 2 * c + 2)
                gp.tensor_tensor(res[k][:, sl, :], h[k][:, sl, :], xn[k][:, sl, 0, :], ALU.add).then_inc(s_res, 1)

            pool.wait_ge(const_edge, 4)
            pool.wait_ge(in_l0, N_L0)
            gp.tensor_copy(WoR[:, :, :, :].rearrange("o (u n) e i -> o u (n e) i", u=2),
                           Wo0[:, :].rearrange("o (i n u) -> o u n i", n=4, u=2)).then_inc(s_wor, 1)
            power(0, 0)
            pool.wait_ge(in_l1, N_L1)
            pool.wait_ge(const_l1, 7)
            gp.tensor_scalar(WqP[:, :, :].rearrange("d g (h k) -> d g h k", h=4)[:, :, :, 0:HD],
                             Wq1[:, :].rearrange("d (g h k) -> d g h k", g=2, h=4), SC0, None, ALU.mult).then_inc(padded, 1)
            power(0, 1)
            gp.tensor_copy(WkP[:, :, :].rearrange("d g (h k) -> d g h k", h=4)[:, :, :, 0:HD],
                           Wk1[:, :].rearrange("d (g h k) -> d g h k", g=2, h=4)).then_inc(padded, 1)
            pool.wait_ge(s_edge, 1)
            gp.indirect_dma_start(out=attr[:, 0:3], out_offset=None, in_=I["L1_attn_edge_attr"],
                                  in_offset=bass.IndirectOffsetOnAxis(ap=edge_u[:, 0:1], axis=0)).then_inc(in_attr, 16)
            for s in range(SLOTS - 1):
                pool.wait_ge(s_rinv, s + 1)
                if s == 0:
                    pool.wait_ge(s_wt_ev, 2)
                for u in range(2):
                    gp.tensor_tensor(WoS[:, s, 4 * u:4 * u + 4, :].rearrange("p (b n) d -> p b n d", b=2),
                                     bc(WoT[:, 2 * u:2 * u + 2, :], 1, 2),
                                     bc(top0[:, 2, s, 4 * u:4 * u + 4].rearrange("p (b n) -> p b n", b=2), 3, D),
                                     ALU.mult).then_inc(s_wos, 1)
            power(1, 0)
            power(1, 1)
            residual(1, 0)
            residual(1, 1)
            power(2, 0)
            power(2, 1)
            for c in range(2):
                sl = slice(2 * c, 2 * c + 2)
                gp.tensor_tensor(res[2][:, sl, :], h[2][:, sl, :], bc(bo_rep[:, :], 1, 2), ALU.add).then_inc(s_h2b, 1)
            power(3, 0)
            power(3, 1)
            residual(3, 0)
            residual(3, 1)
            pool.wait_ge(s_lgd, 1)
            pool.wait_ge(const_sel, 7)
            gp.tensor_tensor(lge[:, :, :].rearrange("p s e -> p (s e)"), euler[:, :],
                             lgd[:, :, :].rearrange("p s e -> p (s e)"), ALU.pow).then_inc(s_lge, 1)

        @block.scalar
        def _(act):
            sc = nc.scalar
            load_x(act, 1, 0)
            act.wait_ge(wbd_zero, 2)
            act.dma_start(Wbd[KROWS:2 * KROWS, :, 1, :], wp_v).then_inc(in_wp, 16)
            load_x(act, 1, 1)

            def layer_xT(k, c):
                n = 2 * k + c
                rows_ = P if k == 0 else D
                act.wait_ge(s_xt, n + 1)
                sc.activation(xT[k][0:rows_, c * HALF:(c + 1) * HALF], B[c][0:rows_, 0:HALF], ACT.Copy).then_inc(s_xt_ev, 1)

            act.wait_ge(s_posh, 1)
            sc.activation(posh[:, :], B[4][0:D, 0:TOK], ACT.Relu).then_inc(s_posh_ev, 1)
            sc.activation(cols[:, :], B[4][:, 64:72], ACT.Copy).then_inc(s_cols_ev, 1)
            sc.activation(qk_cols[:, 0:2], B[4][:, 72:74], ACT.Copy, scale=SC0).then_inc(s_cols_ev, 1)
            sc.activation(qk_cols[:, 2:4], B[4][:, 74:76], ACT.Copy).then_inc(s_cols_ev, 1)
            for c in range(2):
                act.wait_ge(s_nat, c + 1)
                sc.activation(h[0][:, 2 * c:2 * c + 2, :].rearrange("p s d -> p (s d)"), B[2 + c][:, 0:P],
                              ACT.Copy).then_inc(s_h0, 1)
                if c == 0:
                    act.wait_ge(s_wt, 1)
                    sc.activation(wvT[:, :, :], bc(B[5][0:D, 0:64], 1, 2), ACT.Copy).then_inc(s_wt_ev, 1)
                    sc.activation(WoT[:, :, :].rearrange("p q d -> p (q d)"), B[5][:, 256:512], ACT.Copy).then_inc(s_wt_ev, 1)
                    sc.activation(rwT[:, :], B[5][0:D, 64:72], ACT.Copy).then_inc(s_wt_ev, 1)
                    act.wait_ge(s_g, 1)
                    sc.activation(G[:, 0:HEADS:2, :], B[6][0:D, 0:256].rearrange("p (q c) -> p q c", c=D), ACT.Copy).then_inc(s_g_ev, 1)
                    sc.activation(G[:, 1:HEADS:2, :], B[3][0:D, 0:256].rearrange("p (q c) -> p q c", c=D), ACT.Copy).then_inc(s_g_ev, 1)
                layer_xT(0, c)
                for u in range(2):
                    act.wait_ge(s_q0, 2 * c + u + 1)
                    bank = (B[4], B[5], B[6], B[2])[2 * c + u]
                    sc.activation(qT0[:, u, 4 * c:4 * c + 4, :, :].rearrange("p b q n -> p q b n"),
                                  bank[:, :].rearrange("p (q b n) -> p q b n", q=2, n=TOK), ACT.Copy).then_inc(s_q0_ev, 1)
            act.wait_ge(s_v0, 1)
            sc.activation(v0[:, :], B[3][:, :], ACT.Copy).then_inc(s_v0_ev, 1)
            for s in range(SLOTS):
                act.wait_ge(s_sub0, s + 1)
                sc.activation(E0[:, s, :, :], E0[:, s, :, :], ACT.Exp, scale=SC0).then_inc(s_exp0, 1)
                if s in (0, 1):
                    continue
            sc.preload_act_table(ACT.Gelu_apprx_tanh)
            for c in range(2):
                act.wait_ge(s_m0, c + 1)
                bank = (B[6], B[2])[c]
                sc.activation(M0[:, 2 * c:2 * c + 2, :].rearrange("p s d -> p (s d)"), bank[:, 0:P], ACT.Copy).then_inc(s_m0_ev, 1)
            layer_xT(1, 0)
            layer_xT(1, 1)
            for c in range(2):
                act.wait_ge(s_hid, c + 1)
                for k in range(2):
                    sc.activation(hid[:, k, c * HALF:(c + 1) * HALF], B[4 + c][:, k * HALF:(k + 1) * HALF],
                                  ACT.Gelu_apprx_tanh, bias=cols[:, 2 + k:3 + k]).then_inc(s_gelu, 1)
            sc.preload_act_table(ACT.Exp)
            layer_xT(2, 0)
            layer_xT(2, 1)
            for c in range(2):
                act.wait_ge(s_q1, c + 1)
                for g in range(2):
                    sc.activation(qT1[:, g, c * HALF:(c + 1) * HALF], B[4 + 2 * c][:, g * HALF:(g + 1) * HALF],
                                  ACT.Identity, bias=qk_cols[:, g:g + 1]).then_inc(s_q1_ev, 1)

            def exp1(s):
                act.wait_ge(s_sub1, s + 1)
                sc.activation(E1[:, s, :, :], E1[:, s, :, :], ACT.Exp).then_inc(s_exp1, 1)

            def et_copy(s):
                act.wait_ge(s_et, s + 1)
                bank = B[(1, 2, 3, 6)[s]]
                sc.activation(ET[:, s, :, :].rearrange("p q n -> p (q n)"), bank[:, :], ACT.Copy).then_inc(s_et_ev_a, 1)

            exp1(0)
            exp1(1)
            et_copy(0)
            et_copy(1)
            exp1(2)
            exp1(3)
            et_copy(2)
            sc.preload_act_table(ACT.Gelu)
            for c in range(2):
                act.wait_ge(s_ctxT, c + 1)
                bank = (B[7], B[0])[c]
                sc.activation(ctxT[:, c * HALF:(c + 1) * HALF], bank[0:D, 0:HALF], ACT.Copy).then_inc(s_ctxT_ev, 1)
            layer_xT(3, 0)
            layer_xT(3, 1)
            for q in range(4):
                act.wait_ge(s_eh, q + 1)
                sc.activation(ge[:, q, :], B[4 + q][:, :], ACT.Gelu, bias=cols[:, 4 + q:5 + q]).then_inc(s_eg, 1)
            act.wait_ge(s_ct, 1)
            sc.activation(combT[:, :], B[4][0:EXPERTS, :], ACT.Copy).then_inc(s_ct_ev, 1)
            act.wait_ge(s_fin, 1)
            act.wait_ge(s_out_v, 1)
            sc.activation(h[4][:, 2:4, :].rearrange("p s d -> p (s d)"), B[5][:, P:2 * P], ACT.Copy).then_inc(s_out_a, 1)

        @block.vector
        def _(dve):
            ve = nc.vector
            step = [0]

            def link(ins):
                step[0] += 1
                ins.then_inc(s_vec, 1)
                dve.wait_ge(s_vec, step[0])

            ve.memset(Wbd[:, PATCH // 2:PATCH, :, :], 0.0).then_inc(wbd_zero, 1)
            dve.wait_ge(in_ids, 16)
            link(ve.tensor_scalar(idf[:, 0, :], ids[:, :], 0.0, float(TOK), ALU.is_lt, ALU.mult))
            link(ve.tensor_tensor(idf[:, 1, :], ids[:, :], idf[:, 0, :], ALU.add))
            link(ve.tensor_scalar(idf[:, 2, :], idf[:, 1, :], float(TOK), -1.0, ALU.min, ALU.max))
            for k in range(4):
                ins = ve.tensor_scalar(idb[:, k, :], idf[:, 2, :], float(-16 * k), None, ALU.add)
            link(ins)
            dve.wait_ge(const_edge, 1)
            for k in range(4):
                ve.tensor_tensor(onehot[:, 16 * k:16 * k + 16, :], bc(idb[:, k, :], 1, 16), iota16[:, :, :],
                                 ALU.is_equal).then_inc(s_hot, 1)

            def ln_stats(k, c):
                for s in (2 * c, 2 * c + 1):
                    ve.bn_stats(stats[:, k, s, :], h[k][:, s, :]).then_inc(s_st, 1)
                for s in (2 * c, 2 * c + 1):
                    dve.wait_ge(s_st, 4 * k + s + 1)
                    ve.bn_aggr(mv[:, k, s, :], stats[:, k, s, :]).then_inc(s_mv, 1)
                dve.wait_ge(s_mv, 4 * k + 2 * c + 2)
                ve.tensor_scalar(var[:, k, 2 * c:2 * c + 2], mv[:, k, 2 * c:2 * c + 2, 1], EPS, None,
                                 ALU.add).then_inc(s_var, 1)

            def ln_norm(k, c):
                dve.wait_ge(s_rstd, 2 * k + c + 1)
                for s in (2 * c, 2 * c + 1):
                    copies = 2 if k == 0 else 1
                    ins = ve.tensor_scalar(xn[k][:, s, 0:copies, :], bc(h[k][:, s, :], 1, copies), mv[:, k, s, 0:1],
                                           rstd[:, k, s:s + 1], ALU.subtract, ALU.mult)
                ins.then_inc(s_xn, 1)

            dve.wait_ge(s_pos, 1)
            dve.wait_ge(s_cols_ev, 1)
            ve.tensor_scalar(pos[:, :], B[4][:, 128:128 + TOK], cols[:, 0:1], cols[:, 1:2], ALU.add, ALU.add).then_inc(s_pos_ev, 1)
            dve.wait_ge(s_pos_ev, 1)
            for c in range(2):
                dve.wait_ge(s_emb, c + 1)
                ve.tensor_tensor(embT[:, c, :].rearrange("p (b n) -> p b n", b=2),
                                 B[c][:, 0:P].rearrange("p (b n) -> p b n", b=2), bc(pos[:, :], 1, 2),
                                 ALU.add).then_inc(s_embT, 1)
                dve.wait_ge(s_h0, c + 1)
                ln_stats(0, c)
                ln_norm(0, c)

            dve.wait_ge(s_expo, 4)
            dve.wait_ge(const_edge, 4)
            link(ve.tensor_scalar(expo[:, :, :], B[7][:, 0:2 * TOK].bitcast(i32).rearrange("p (j u) -> p j u", u=2),
                                  23, None, ALU.logical_shift_right))
            link(ve.tensor_scalar(last[:, 0, :], expo[:, :, 1], 0.0, 128.0, ALU.is_gt, ALU.mult))
            link(ve.tensor_tensor(last[:, 1, :], last[:, 0, :], expo[:, :, 1], ALU.add))
            link(ve.tensor_tensor(last[:, 2, :], last[:, 1, :], expo[:, :, 0], ALU.max))
            ve.tensor_scalar(last[:, 0, :], last[:, 2, :], float(D), col_idx[:, 0:1], ALU.mult, ALU.add).then_inc(s_key, 1)

            def softmax0_shift(s):
                c, j = s // 2, s % 2
                S = psum[:, 4 * c:4 * c + 2, j * 256:(j + 1) * 256].rearrange("p u (q t) -> p u q t", t=TOK)
                top = top0[:, 0, s, :].rearrange("p (u q) -> p u q", u=2)
                dve.wait_ge(s_sc0, c + 1)
                ve.tensor_reduce(top, S, X, ALU.max).then_inc(s_mx0, 1)
                dve.wait_ge(s_mx0, s + 1)
                ve.tensor_tensor(E0[:, s, :, :].rearrange("p (u q) t -> p u q t", u=2), S, bc(top, 3, TOK),
                                 ALU.subtract).then_inc(s_sub0, 1)

            def softmax0_sum(s):
                dve.wait_ge(s_exp0, s + 1)
                ve.tensor_reduce(top0[:, 1, s, :], E0[:, s, :, :], X, ALU.add).then_inc(s_sum0, 1)
                dve.wait_ge(s_sum0, s + 1)
                ve.reciprocal(top0[:, 2, s, :], top0[:, 1, s, :]).then_inc(s_rinv, 1)

            softmax0_shift(0)
            softmax0_shift(1)
            softmax0_sum(0)
            softmax0_sum(1)
            dve.wait_ge(s_keyT, 1)
            link(ve.tensor_reduce(edge[:, 0:1], B[7][0:TOK, 256:256 + P], X, ALU.max))
            link(ve.tensor_scalar(edge[:, 1:2], edge[:, 0:1], float(ABSENT), None, ALU.is_ge))
            link(ve.tensor_scalar(edge_u[:, 0:1], edge[:, 0:1], float(-ABSENT), 0.0, ALU.add, ALU.max))
            dve.sem_inc(s_edge, 1)
            softmax0_shift(2)
            softmax0_shift(3)
            softmax0_sum(2)
            softmax0_sum(3)
            dve.wait_ge(s_rinv, 4)
            for u in range(2):
                ve.tensor_tensor(WoS[:, 3, 4 * u:4 * u + 4, :].rearrange("p (b n) d -> p b n d", b=2),
                                 bc(WoT[:, 2 * u:2 * u + 2, :], 1, 2),
                                 bc(top0[:, 2, 3, 4 * u:4 * u + 4].rearrange("p (b n) -> p b n", b=2), 3, D),
                                 ALU.mult).then_inc(s_wosd, 1)
            for c in range(2):
                dve.wait_ge(s_o0, c + 1)
                sl = slice(2 * c, 2 * c + 2)
                ve.tensor_tensor(h[1][:, sl, :], h[0][:, sl, :], (B[3], B[7])[c][:, 0:P].rearrange("p (s d) -> p s d", s=2),
                                 ALU.add).then_inc(s_h, 1)
                dve.wait_ge(s_h, c + 1)
                ln_stats(1, c)
            ln_norm(1, 0)
            ln_norm(1, 1)
            dve.wait_ge(s_attrT, 1)
            ve.tensor_copy(attrT[:, :], B[7][0:4, 256:256 + TOK]).then_inc(s_attrT_ev, 1)

            dve.wait_ge(s_wr, 1)
            dve.wait_ge(in_f0, N_F0)
            dve.wait_ge(const_sel, 7)
            link(ve.tensor_scalar(wall[:, :, :].rearrange("p s n -> p (s n)"), B[6][:, 0:256], br[:, 0:1], None, ALU.add))
            link(ve.tensor_tensor(wdiag[:, :, :], wall[:, :, :], bc(eye2[:, :], 1, SLOTS), ALU.mult))
            link(ve.tensor_reduce(wcol[:, :], wdiag[:, :, :], X, ALU.add))
            for s in range(SLOTS):
                ins = ve.scalar_tensor_tensor(tie[:, s, :], wall[:, s, :], wcol[:, s:s + 1], earlier[:, :],
                                              ALU.is_equal, ALU.mult)
            link(ins)
            for s in range(SLOTS):
                ins = ve.scalar_tensor_tensor(ahead[:, s, :], wall[:, s, :], wcol[:, s:s + 1], tie[:, s, :],
                                              ALU.is_gt, ALU.add, accum_out=rank[:, s:s + 1])
            link(ins)
            link(ve.scalar_tensor_tensor(gate[:, :], rank[:, :], float(KSEL), wcol[:, :], ALU.is_lt, ALU.mult))
            dve.wait_ge(s_eb, 1)
            dve.wait_ge(const_l1, 3)
            ve.tensor_scalar(biasP[:, :, :].rearrange("j g (h k) -> j g h k", h=4)[:, :, :, HD:HD + 1].rearrange("j g h k -> j g (h k)"),
                             B[7][0:TOK, 448:456].rearrange("j (g h) -> j g h", g=2), edge[:, 1:2], None, ALU.mult).then_inc(s_biasP, 1)
            for c in range(2):
                dve.wait_ge(s_y, c + 1)
                dve.wait_ge(s_res, c + 1)
                for j in range(2):
                    s = 2 * c + j
                    ins = ve.scalar_tensor_tensor(h[2][:, s, :], (B[2], B[3])[c][:, j * D:(j + 1) * D], gate[:, s:s + 1],
                                                  res[1][:, s, :], ALU.mult, ALU.add)
                ins.then_inc(s_h, 1)
                dve.wait_ge(s_h, 2 + c + 1)
                ln_stats(2, c)
            ln_norm(2, 0)
            ln_norm(2, 1)
            dve.wait_ge(s_kb, 1)
            for g in range(2):
                ins = ve.tensor_scalar(kbias[:, g, :], B[7][:, 320 + g * TOK:320 + (g + 1) * TOK], qk_cols[:, 2 + g:3 + g],
                                       None, ALU.add)
            ins.then_inc(s_kb_ev, 1)
            dve.wait_ge(s_kb_ev, 1)
            for c in range(2):
                dve.wait_ge(s_k1, c + 1)
                for g in range(2):
                    ve.tensor_tensor(kT1[:, g, c * HALF:(c + 1) * HALF].rearrange("p (b n) -> p b n", n=TOK),
                                     B[5 + 2 * c][:, g * HALF:(g + 1) * HALF].rearrange("p (b n) -> p b n", n=TOK),
                                     bc(kbias[:, g, :], 1, 4), ALU.add).then_inc(s_k1_ev, 1)
            dve.wait_ge(const_l1, 7)

            def softmax1_shift(s):
                c, j = s // 2, s % 2
                S = psum[:, 4 * c:4 * c + 4, j * P:(j + 1) * P].rearrange("p q (g t) -> p q g t", t=TOK)
                top = top1[:, s, :].rearrange("p (q g) -> p q g", g=2)
                dve.wait_ge(s_sc1, c + 1)
                ve.tensor_reduce(top, S, X, ALU.max).then_inc(s_mx1, 1)
                dve.wait_ge(s_mx1, s + 1)
                ve.tensor_tensor(E1[:, s, :, :].rearrange("p (q g) t -> p q g t", g=2), S, bc(top, 3, TOK),
                                 ALU.subtract).then_inc(s_sub1, 1)

            for s in range(SLOTS):
                softmax1_shift(s)
            dve.wait_ge(s_v1, 1)
            for u in range(2):
                half = slice(u * TOK, (u + 1) * TOK)
                ins = ve.tensor_tensor(vB[half, :, :, u * (HD + 1):u * (HD + 1) + HD],
                                       B[0][half, :].rearrange("p (b q k) -> p b q k", b=BATCH, k=HD)[:, :, 4 * u:4 * u + 4, :],
                                       bc(bv_rep[half, :].rearrange("p (q k) -> p q k", k=HD)[:, 4 * u:4 * u + 4, :], 1, BATCH),
                                       ALU.add)
            ins.then_inc(s_v1_ev, 1)
            dve.wait_ge(s_et, 4)
            ve.tensor_copy(ET[:, 3, :, :].rearrange("p q n -> p (q n)"), B[6][:, :]).then_inc(s_et_ev_v, 1)
            for c in range(2):
                sl = slice(2 * c, 2 * c + 2)
                C = (B[4], B[5])[c][:, 0:2 * HEADS * (HD + 1)].rearrange("p (s q k) -> p s q k", s=2, k=HD + 1)
                dve.wait_ge(s_av, c + 1)
                link(ve.reciprocal(rden[:, sl, :], C[:, :, :, HD]))
                for g in range(2):
                    ins = ve.tensor_tensor(ctxn[:, sl, 32 * g:32 * g + 32].rearrange("p s (q k) -> p s q k", k=HD),
                                           C[:, :, g:HEADS:2, 0:HD], bc(rden[:, sl, g:HEADS:2], 3, HD), ALU.mult)
                ins.then_inc(s_ctx, 1)
            for c in range(2):
                sl = slice(2 * c, 2 * c + 2)
                dve.wait_ge(s_o1, c + 1)
                dve.wait_ge(s_h2b, c + 1)
                ve.tensor_tensor(h[3][:, sl, :], res[2][:, sl, :], (B[1], B[2])[c][:, 0:P].rearrange("p (s d) -> p s d", s=2),
                                 ALU.add).then_inc(s_h, 1)
                dve.wait_ge(s_h, 4 + c + 1)
                ln_stats(3, c)
            ln_norm(3, 0)
            ln_norm(3, 1)

            dve.wait_ge(s_lg, 1)
            link(ve.tensor_copy(lg[:, :, :].rearrange("p s e -> p (s e)"), B[3][:, 0:SLOTS * EXPERTS]))
            link(ve.tensor_reduce(lgm[:, :], lg[:, :, :], X, ALU.max))
            ve.tensor_tensor(lgd[:, :, :], lg[:, :, :], bc(lgm[:, :], 2, EXPERTS), ALU.subtract).then_inc(s_lgd, 1)
            other = bc(lg[:, :, :], 2, EXPERTS)
            own = bc(lg[:, :, :], 3, EXPERTS)
            bt = [better[:, n, :, :].rearrange("p (s e) f -> p s e f", e=EXPERTS) for n in range(3)]
            link(ve.tensor_tensor(bt[0], other, own, ALU.is_equal))
            link(ve.tensor_tensor(bt[1], bt[0], bc(earlier8[:, :, :], 1, SLOTS), ALU.mult))
            link(ve.tensor_tensor(bt[2], other, own, ALU.is_gt))
            link(ve.tensor_tensor(bt[0], bt[1], bt[2], ALU.add))
            link(ve.tensor_reduce(erank[:, :], better[:, 0, :, :], X, ALU.add))
            dve.wait_ge(s_lge, 1)
            link(ve.scalar_tensor_tensor(esel[:, :, :].rearrange("p s e -> p (s e)"), erank[:, :], 2.0,
                                         lge[:, :, :].rearrange("p s e -> p (s e)"), ALU.is_lt, ALU.mult))
            link(ve.tensor_reduce(esum[:, 0, :], esel[:, :, :], X, ALU.add))
            link(ve.reciprocal(esum[:, 1, :], esum[:, 0, :]))
            ve.tensor_tensor(comb[:, :, :], esel[:, :, :], bc(esum[:, 1, :], 2, EXPERTS), ALU.mult).then_inc(s_comb, 1)
            dve.wait_ge(s_comb, 1)
            link(ve.tensor_copy(comb3[:, :, 0, :], comb[:, :, :]))
            link(ve.tensor_tensor(part[:, 0, :, :], comb[:, :, :], comb3[:, :, 0, :], ALU.subtract))
            link(ve.tensor_copy(comb3[:, :, 1, :], part[:, 0, :, :]))
            link(ve.tensor_tensor(part[:, 1, :, :], part[:, 0, :, :], comb3[:, :, 1, :], ALU.subtract))
            ve.tensor_copy(comb3[:, :, 2, :], part[:, 1, :, :]).then_inc(s_comb, 1)
            dve.wait_ge(s_c3, 1)
            ve.tensor_copy(comb3T[:, :], C3[:, :]).then_inc(s_c3_ev, 1)
            for q in range(4):
                dve.wait_ge(s_eg, q + 1)
                dve.wait_ge(s_cr, q + 1)
                ve.tensor_tensor(gs[:, q, :], ge[:, q, :], (B[2], B[1], B[0], B[3])[q][:, :], ALU.mult).then_inc(s_gs, 1)
            dve.wait_ge(s_fin, 1)
            ve.tensor_copy(h[4][:, 0:2, :].rearrange("p s d -> p (s d)"), B[5][:, 0:P]).then_inc(s_out_v, 1)

        @block.tensor
        def _(pe):
            mm = nc.tensor.matmul

            def tr(o, i, n):
                return nc.tensor.transpose(o, i, ident[0:n, 0:n])

            pe.wait_ge(in_pos, N_POS)
            pe.wait_ge(const_id, 1)
            pe.wait_ge(in_rows, N_ROWS)
            mm(B[4][0:D, 0:TOK], lhsT=posW1[:, :], rhs=gridT[:, :], start=True, stop=True)
            tr(B[4][:, 64:72], rows[:, :], 8)
            tr(B[4][:, 72:76], qk_rows[:, :], 4).then_inc(s_posh, 1)

            def embed(c):
                pe.wait_ge(in_x[c], 2 * 2 * CH * 16)
                pe.wait_ge(in_wp, 32)
                for w in range(PATCH):
                    rhs = Xt[:, 2 * c:2 * c + 2, :, :].rearrange("k b y (q w) -> k (b y) q w", w=PATCH)[:, :, :, w]
                    ins = mm(B[c][:, 0:P], lhsT=Wbd[0:2 * KROWS, w, :, :], rhs=rhs, start=(w == 0), stop=(w == PATCH - 1))
                ins.then_inc(s_emb, 1)

            def natural(c):
                pe.wait_ge(s_embT, c + 1)
                tr(B[2 + c][:, 0:P], embT[:, c, :], P).then_inc(s_nat, 1)

            def last_rows(k):
                pe.wait_ge(s_hot, k + 1)
                pe.wait_ge(const_edge, 2)
                for j in range(16 * k, 16 * k + 16):
                    ins = mm(B[7][:, 2 * j:2 * j + 2], lhsT=onehot[:, j, :], rhs=row_pow[:, :], start=True, stop=True)
                ins.then_inc(s_expo, 1)

            def layer_xT(k, c):
                pe.wait_ge(s_xn, 2 * k + c + 1)
                for j in range(2):
                    s = 2 * c + j
                    if k == 0:
                        ins = tr(B[c][:, j * P:(j + 1) * P], xn[k][:, s, :, :], P)
                    else:
                        ins = tr(B[c][0:D, j * P:(j + 1) * P], xn[k][:, s, 0, :], P)
                ins.then_inc(s_xt, 1)

            embed(0)
            pe.wait_ge(s_posh_ev, 1)
            pe.wait_ge(s_cols_ev, 3)
            mm(B[4][:, 128:128 + TOK], lhsT=posW2[:, :, :], rhs=posh[:, :], start=True, stop=True).then_inc(s_pos, 1)
            natural(0)
            pe.wait_ge(in_l0, N_L0)
            pe.wait_ge(s_wor, 1)
            tr(B[5][0:D, 0:64], Wv0[:, :], D)
            tr(B[5][0:D, 64:72], rw[:, :], EXPERTS)
            for q in range(4):
                ins = tr(B[5][:, 256 + q * D:256 + (q + 1) * D], WoR[:, q, :, :], D)
            ins.then_inc(s_wt, 1)
            for k in range(4):
                mm(B[6][0:D, k * D:(k + 1) * D], lhsT=Wq0[0:D, k, :], rhs=Wk0[0:D, :], start=True, stop=True)
                ins = mm(B[3][0:D, k * D:(k + 1) * D], lhsT=Wq0[D:P, k, :], rhs=Wk0[D:P, :], start=True, stop=True)
            ins.then_inc(s_g, 1)
            embed(1)
            pe.wait_ge(s_g_ev, 2)
            natural(1)
            layer_xT(0, 0)

            def queries0(c):
                pe.wait_ge(s_xt_ev, c + 1)
                for u in range(2):
                    if c == 0:
                        pe.wait_ge((s_pos_ev, s_wt_ev)[u], (1, 3)[u])
                    bank = (B[4], B[5], B[6], B[2])[2 * c + u]
                    for q in range(2):
                        ins = mm(bank[:, q * HALF:(q + 1) * HALF], lhsT=G[:, 4 * u + 2 * q:4 * u + 2 * q + 2, :],
                                 rhs=xT[0][0:D, c * HALF:(c + 1) * HALF], start=True, stop=True)
                    ins.then_inc(s_q0, 1)

            def scores0(c):
                pe.wait_ge(s_q0_ev, 2 * c + 2)
                for j in range(2):
                    for b in range(2):
                        tok = c * HALF + j * P + b * TOK
                        for n in range(2):
                            for par in range(2):
                                q = 4 * j + 2 * b + n
                                ins = mm(B[4 * c + par][:, q * TOK:(q + 1) * TOK],
                                         lhsT=qT0[par * D:(par + 1) * D, n, 4 * c + 2 * j + b, :, :],
                                         rhs=xT[0][par * D:(par + 1) * D, tok:tok + TOK], start=True, stop=True)
                ins.then_inc(s_sc0, 1)

            for k in range(4):
                last_rows(k)
            queries0(0)
            layer_xT(0, 1)
            pe.wait_ge(s_xt_ev, 2)
            scores0(0)
            queries0(1)
            mm(B[3][:, :], lhsT=wvT[:, :, :], rhs=xT[0][0:D, :], start=True, stop=True).then_inc(s_v0, 1)
            pe.wait_ge(s_key, 1)
            tr(B[7][0:TOK, 256:256 + P], last[:, 0, :], P).then_inc(s_keyT, 1)
            scores0(1)
            for c in range(2):
                bank = (B[6], B[2])[c]
                for j in range(2):
                    s = 2 * c + j
                    pe.wait_ge(s_exp0, s + 1)
                    if s < 3:
                        pe.wait_ge(s_wos, 2 * s + 2)
                    else:
                        pe.wait_ge(s_wosd, 2)
                    if s == 0:
                        pe.wait_ge(s_q0_ev, 4)
                    for q in range(4):
                        for b in range(2):
                            ins = mm(bank[b * D:(b + 1) * D, j * D:(j + 1) * D], lhsT=E0[:, s, 4 * (q // 2) + 2 * b + q % 2, :],
                                     rhs=WoS[:, s, 4 * (q // 2) + 2 * b + q % 2, :], start=(q == 0), stop=(q == 3))
                ins.then_inc(s_m0, 1)
                pe.wait_ge(s_m0_ev, c + 1)
                pe.wait_ge(s_v0_ev, 1)
                if c == 1:
                    pe.wait_ge(s_edge, 1)
                for b in range(2):
                    for j in range(2):
                        tok = c * HALF + j * P + b * TOK
                        ins = mm((B[3], B[7])[c][b * D:(b + 1) * D, j * D:(j + 1) * D], lhsT=v0[b * D:(b + 1) * D, tok:tok + TOK],
                                 rhs=M0[b * D:(b + 1) * D, 2 * c + j, :], start=True, stop=True)
                ins.then_inc(s_o0, 1)

            pe.wait_ge(in_f0, N_F0)
            layer_xT(1, 0)
            layer_xT(1, 1)
            pe.wait_ge(s_h, 2)
            pe.wait_ge(in_attr, 16)
            tr(B[7][0:4, 256:256 + TOK], attr[:, :], TOK).then_inc(s_attrT, 1)
            for c in range(2):
                pe.wait_ge(s_xt_ev, 2 + c + 1)
                for k in range(2):
                    ins = mm(B[4 + c][:, k * HALF:(k + 1) * HALF], lhsT=w1f[:, k * P:(k + 1) * P],
                             rhs=xT[1][0:D, c * HALF:(c + 1) * HALF], start=True, stop=True)
                ins.then_inc(s_hid, 1)
            for b in range(2):
                rhs = xT[1][0:D, :].rearrange("d (s b n) -> d s b n", b=2, n=TOK)[:, :, b, :]
                ins = mm(B[6][b * D:(b + 1) * D, 0:256], lhsT=wr[:, 0:1].broadcast_to([D, D]), rhs=rhs, start=True, stop=True)
            ins.then_inc(s_wr, 1)
            pe.wait_ge(s_attrT_ev, 1)
            mm(B[7][0:TOK, 448:456], lhsT=attrT[:, :], rhs=WeB[:, :], start=True, stop=True).then_inc(s_eb, 1)
            for c in range(2):
                pe.wait_ge(s_gelu, 2 * c + 2)
                for j in range(2):
                    s = 2 * c + j
                    o = (B[2], B[3])[c][:, j * D:(j + 1) * D]
                    for k in range(2):
                        mm(o, lhsT=hid[:, k, s * P:(s + 1) * P], rhs=w2f[:, k, :], start=(k == 0), stop=False)
                    ins = mm(o, lhsT=ones_row[:, :], rhs=b2f[:, :], start=False, stop=True)
                ins.then_inc(s_y, 1)
            pe.wait_ge(s_biasP, 1)
            for g in range(2):
                ins = mm(B[7][:, 320 + g * TOK:320 + (g + 1) * TOK], lhsT=biasP[:, g, :], rhs=ident[0:TOK, 0:TOK],
                         start=True, stop=True)
            ins.then_inc(s_kb, 1)

            layer_xT(2, 0)
            layer_xT(2, 1)
            pe.wait_ge(padded, 2)
            for c in range(2):
                pe.wait_ge(s_xt_ev, 4 + c + 1)
                src = xT[2][0:D, c * HALF:(c + 1) * HALF]
                for g in range(2):
                    ins = mm(B[4 + 2 * c][:, g * HALF:(g + 1) * HALF], lhsT=WqP[:, g, :], rhs=src, start=True, stop=True)
                ins.then_inc(s_q1, 1)
                if c == 1:
                    pe.wait_ge(s_kb_ev, 1)
                for g in range(2):
                    ins = mm(B[5 + 2 * c][:, g * HALF:(g + 1) * HALF], lhsT=WkP[:, g, :], rhs=src, start=True, stop=True)
                ins.then_inc(s_k1, 1)

            def scores1(c):
                pe.wait_ge(s_q1_ev, 2 * c + 2 if c == 0 else 4)
                pe.wait_ge(s_k1_ev, 2 * c + 2)
                for j in range(2):
                    for g in range(2):
                        col = (2 * j + g) * TOK
                        for hh in range(4):
                            rows_ = slice(32 * hh, 32 * hh + HD + 1)
                            for b in range(2):
                                tok = c * HALF + j * P + b * TOK
                                ins = mm(B[4 * c + hh][b * D:(b + 1) * D, col:col + TOK], lhsT=qT1[rows_, g, tok:tok + TOK],
                                         rhs=kT1[rows_, g, tok:tok + TOK], start=True, stop=True)
                ins.then_inc(s_sc1, 1)

            def values1():
                pe.wait_ge(s_sub1, 2)
                for b in range(BATCH):
                    for u in range(2):
                        ins = mm(B[0][u * D:(u + 1) * D, b * D:(b + 1) * D], lhsT=xT[2][0:D, b * TOK:(b + 1) * TOK],
                                 rhs=Wv1[:, :], start=True, stop=True)
                ins.then_inc(s_v1, 1)

            def probsT(s):
                pe.wait_ge(s_exp1, s + 1)
                bank = B[(1, 2, 3, 6)[s]]
                for q in range(4):
                    ins = tr(bank[:, q * P:(q + 1) * P], E1[:, s, 2 * q:2 * q + 2, :], P)
                ins.then_inc(s_et, 1)

            def context(c):
                for j in range(2):
                    s = 2 * c + j
                    if s < 3:
                        pe.wait_ge(s_et_ev_a, s + 1)
                    else:
                        pe.wait_ge(s_et_ev_v, 1)
                    for q in range(4):
                        for b in range(2):
                            col = (j * 4 + q) * 2 * (HD + 1)
                            ins = mm((B[4], B[5])[c][b * D:(b + 1) * D, col:col + 2 * (HD + 1)],
                                     lhsT=ET[:, s, q, b * TOK:(b + 1) * TOK], rhs=vB[:, 2 * s + b, q, :], start=True, stop=True)
                ins.then_inc(s_av, 1)

            scores1(0)
            scores1(1)
            values1()
            probsT(0)
            probsT(1)
            probsT(2)
            pe.wait_ge(s_v1_ev, 1)
            pe.wait_ge(s_sub1, 4)
            context(0)
            probsT(3)
            context(1)
            for c in range(2):
                pe.wait_ge(s_ctx, c + 1)
                for j in range(2):
                    ins = tr((B[7], B[0])[c][0:D, j * P:(j + 1) * P], ctxn[:, 2 * c + j, :], P)
                ins.then_inc(s_ctxT, 1)
            for c in range(2):
                pe.wait_ge(s_ctxT_ev, c + 1)
                for j in range(2):
                    s = 2 * c + j
                    ins = mm((B[1], B[2])[c][:, j * D:(j + 1) * D], lhsT=ctxT[:, s * P:(s + 1) * P], rhs=Wo1[:, :],
                             start=True, stop=True)
                ins.then_inc(s_o1, 1)

            layer_xT(3, 0)
            layer_xT(3, 1)
            pe.wait_ge(in_moe, N_MOE)
            pe.wait_ge(s_xt_ev, 8)
            for s in range(SLOTS):
                ins = mm(B[3][:, s * EXPERTS:(s + 1) * EXPERTS], lhsT=xT[3][0:D, s * P:(s + 1) * P], rhs=rwT[:, :],
                         start=True, stop=True)
            ins.then_inc(s_lg, 1)
            for q in range(4):
                mm(B[4 + q][:, :], lhsT=w1e[:, 2 * q:2 * q + 2, :], rhs=xT[3][0:D, :], start=True, stop=True).then_inc(s_eh, 1)
            pe.wait_ge(s_comb, 2)
            pe.wait_ge(const_moe, 5)
            for s in range(SLOTS):
                ins = nc.tensor.transpose(C3[:, s * P:(s + 1) * P], comb3[:, s, :, :], ident_h[:, :])
            ins.then_inc(s_c3, 1)
            pe.wait_ge(s_c3_ev, 1)
            for q in range(4):
                mm((B[2], B[1], B[0], B[3])[q][:, :], lhsT=sel3[:, q, :], rhs=comb3T[:, :], start=True, stop=True).then_inc(s_cr, 1)
            pe.wait_ge(s_eg, 1)
            for s in range(SLOTS):
                ins = tr(B[4][0:EXPERTS, s * P:(s + 1) * P], comb[:, s, :], P)
            ins.then_inc(s_ct, 1)
            pe.wait_ge(s_eg, 2)
            pe.wait_ge(s_res, 4)
            F = B[5]
            mm(F[:, 0:256], lhsT=ident[:, :], rhs=res[3][:, :, :].rearrange("p s d -> p (s d)"), start=True, stop=True)
            pe.wait_ge(s_ct_ev, 1)
            for s in range(SLOTS):
                mm(F[:, s * D:(s + 1) * D], lhsT=combT[:, s * P:(s + 1) * P], rhs=b2e[:, :], start=False, stop=False,
                   skip_group_check=True)
            for q in range(4):
                pe.wait_ge(s_gs, q + 1)
                for s in range(SLOTS):
                    ins = mm(F[:, s * D:(s + 1) * D], lhsT=gs[:, q, s * P:(s + 1) * P], rhs=w2e[:, q, :], start=False,
                             stop=(q == 3), skip_group_check=True)
            ins.then_inc(s_fin, 1)


_OUTS = [((8, 64, 64), 'float32')]


def kernel(**inputs):
    import numpy as _np
    import concourse.bacc as _bacc
    from concourse import mybir as _mybir
    from concourse.bass_utils import run_bass_kernel_spmd as _run

    nc = _bacc.Bacc("TRN2", target_bir_lowering=False, num_devices=1)
    arrays, args = {}, {}
    for name, value in inputs.items():
        if name == "L0_ffn_attention_mask":
            continue
        a = _np.ascontiguousarray(value)
        arrays[f"in_{name}_dram"] = a
        args[name] = nc.dram_tensor(f"in_{name}_dram", a.shape, _mybir.dt.from_np(a.dtype), kind="ExternalInput").ap()
    n = 8
    grid = _np.ones((3, n * n), _np.float32)
    grid[0] = _np.repeat(_np.arange(n, dtype=_np.float32), n) / _np.float32(n - 1)
    grid[1] = _np.tile(_np.arange(n, dtype=_np.float32), n) / _np.float32(n - 1)
    arrays["grid_dram"] = grid
    grid_ap = nc.dram_tensor("grid_dram", grid.shape, _mybir.dt.from_np(grid.dtype), kind="ExternalInput").ap()
    outs = []
    for i, (shape, dtype) in enumerate(_OUTS):
        dt = _mybir.dt.from_np(_np.dtype(dtype))
        outs.append(nc.dram_tensor(f"out_{i}_dram", shape, dt, kind="ExternalOutput").ap())
    vit_tower(nc, args, grid_ap, outs[0])
    r = _run(nc, [arrays], core_ids=[0])
    return r.results[0]["out_0_dram"]
```

```python
import numpy as np
import concourse.bass as bass
from concourse import mybir
from contextlib import ExitStack


P = 128
BATCH, CH, SIDE, PATCH = 8, 3, 128, 16
NP = SIDE // PATCH
TOK = NP * NP
D = 64
HEADS = 8
HD = D // HEADS
EXPERTS = 8
HID = 4 * D
KX = CH * PATCH * PATCH // P
SC0 = 1.0 / float(np.sqrt(np.float32(8)))
SC0_INV = float(np.nextafter(np.float32(1) / np.float32(SC0), np.float32(4)))

FIELDS = {
    "first": [("Wp", P, KX * D), ("posW2", D + 2, D), ("posW1", 3, D), ("grid", 3, P)],
    "attn0": [("ident", P, P), ("Wq0", P, 4 * D), ("Wk0", P, D), ("WvT", D, 2 * D), ("WoT", P, 4 * D),
              ("col_idx", P, 1), ("row_pow", P, 2)],
    "mid": [("w1f", D, HID), ("w2f", P, HID // P * D), ("b2f", 1, D), ("ones_row", 1, P), ("wr", D, 1), ("br", P, 1),
            ("b1f", P, HID // P), ("eye2", P, TOK), ("earlier", P, TOK), ("Wq1", D, 2 * P), ("Wk1", D, 2 * P),
            ("Wv1", D, D), ("Wo1", D, D), ("bv_rep", P, D), ("bo_rep", P, D), ("We", 4, HEADS),
            ("bq1", P, 2), ("bk1", P, 2)],
    "moe": [("rwT", D, EXPERTS), ("w1e", D, EXPERTS * D), ("w2e", P, EXPERTS // 2 * D), ("b2e", EXPERTS, D),
            ("b1e", P, EXPERTS // 2), ("earlier8", P, EXPERTS * EXPERTS), ("sel3", 3 * EXPERTS, EXPERTS * D)],
}


def width(group):
    return sum(n for _, _, n in FIELDS[group])


def vit_tower(nc, I, packs, out):
    fp32 = mybir.dt.float32
    bf16 = mybir.dt.bfloat16
    i32 = mybir.dt.int32
    u32 = mybir.dt.uint32
    ALU = mybir.AluOpType
    ACT = mybir.ActivationFunctionType
    X = mybir.AxisListType.X

    NT = BATCH * TOK
    SLOTS = NT // P
    HALF = NT // 2
    EDGES = I["L1_attn_edge_index"].shape[1]
    ROWE = EDGES // P
    KSEL = max(1, TOK // 2) - 1
    EPS = 1e-5
    WARM = 12
    EXPO = 127
    ABSENT = D * EXPO

    ctx = ExitStack()
    with ctx:
        def sb(name, shape, dt=fp32):
            return ctx.enter_context(nc.sbuf_tensor(name, shape, dt))

        def sem(name):
            return ctx.enter_context(nc.semaphore(name))

        pack = {g: sb(f"pack_{g}", [P, width(g)]) for g in FIELDS}
        at = {}
        for g, fields in FIELDS.items():
            o = 0
            for name, parts, n in fields:
                at[name] = pack[g][0:parts, o:o + n]
                o += n
        Wp = at["Wp"].rearrange("k (q d) -> k q d", d=D)
        posW2, posW1, grid = at["posW2"], at["posW1"], at["grid"]
        ident = at["ident"]
        Wq0 = at["Wq0"].rearrange("p (k c) -> p k c", c=D)
        Wk0, WvT, col_idx, row_pow_f = at["Wk0"], at["WvT"], at["col_idx"], at["row_pow"]
        WoT = at["WoT"].rearrange("p (q d) -> p q d", d=D)
        w1f, b2f, ones_row, wr, br, b1f = at["w1f"], at["b2f"], at["ones_row"], at["wr"], at["br"], at["b1f"]
        w2f = at["w2f"].rearrange("p (k d) -> p k d", d=D)
        eye2, earlier = at["eye2"], at["earlier"]
        WqP = at["Wq1"].rearrange("d (g n) -> d g n", g=2)
        WkP = at["Wk1"].rearrange("d (g n) -> d g n", g=2)
        Wv1, Wo1, bv_rep, bo_rep, WeB, bq1, bk1 = (at[n] for n in ("Wv1", "Wo1", "bv_rep", "bo_rep", "We", "bq1", "bk1"))
        rwT, b2e, b1e = at["rwT"], at["b2e"], at["b1e"]
        w1e = at["w1e"].rearrange("d (e f) -> d e f", f=D)
        w2e = at["w2e"].rearrange("p (q d) -> p q d", d=D)
        earlier8 = at["earlier8"].rearrange("p (e f) -> p e f", e=EXPERTS)
        Xt = sb("Xt", [P, 2, KX, HALF])
        warm = sb("warm", [P, 512], bf16)
        neg_half = sb("neg_half", [P, SLOTS])
        iota16 = sb("iota16", [P, 16, P], bf16)
        row_pow = sb("row_pow", [P, 2], bf16)
        sel3 = sb("sel3", [3 * EXPERTS, 4, P], bf16)
        ident_h = sb("ident_h", [P, P], bf16)
        bq_scaled = sb("bq_scaled", [P, 2])
        G = sb("G", [D, HEADS, D])
        ids = sb("ids", [P, ROWE], i32)

        idf = sb("idf", [P, 3, ROWE])
        idb = sb("idb", [P, 4, ROWE], bf16)
        onehot = sb("onehot", [P, TOK, ROWE], bf16)
        expo = sb("expo", [P, TOK, 2], i32)
        last = sb("last", [P, 3, TOK])
        edge = sb("edge", [TOK, 4])
        edge_u = sb("edge_u", [TOK, 1], u32)
        attr = sb("attr", [TOK, 4])
        attrT = sb("attrT", [4, TOK])
        biasP = sb("biasP", [TOK, 2, P])
        kbias = sb("kbias", [P, 2, TOK])

        posh = sb("posh", [D + 2, P])
        h = [sb(f"h{i}", [P, SLOTS, D]) for i in range(5)]
        stats = sb("stats", [P, 4, SLOTS, 6])
        mv = sb("mv", [P, 4, SLOTS, 2])
        var = sb("var", [P, 4, SLOTS])
        rstd = sb("rstd", [P, 4, SLOTS])
        xn = [sb(f"xn{i}", [P, SLOTS, 2, D]) for i in range(4)]
        xT = [sb(f"xT{i}", [P, NT]) for i in range(4)]
        res = [sb(f"res{i}", [P, SLOTS, D]) for i in range(4)]
        qT0 = sb("qT0", [P, 2, BATCH, 2, TOK])
        v0 = sb("v0", [P, NT])
        top0 = sb("top0", [P, 3, SLOTS, HEADS])
        E0 = sb("E0", [P, SLOTS, HEADS, TOK])
        WoS = sb("WoS", [P, SLOTS, HEADS, D])
        M0 = sb("M0", [P, SLOTS, D])
        hid = sb("hid", [P, 2, NT])
        wall = sb("wall", [P, SLOTS, TOK])
        wdiag = sb("wdiag", [P, SLOTS, TOK])
        wcol = sb("wcol", [P, SLOTS])
        tie = sb("tie", [P, SLOTS, TOK])
        ahead = sb("ahead", [P, SLOTS, TOK])
        rank = sb("rank", [P, SLOTS])
        gate = sb("gate", [P, SLOTS])
        qT1 = sb("qT1", [P, 2, NT])
        kT1 = sb("kT1", [P, 2, NT])
        vB = sb("vB", [P, BATCH, 4, 2 * (HD + 1)])
        top1 = sb("top1", [P, SLOTS, HEADS])
        E1 = sb("E1", [P, SLOTS, HEADS, TOK])
        ET = sb("ET", [P, SLOTS, 4, P])
        rden = sb("rden", [P, SLOTS, HEADS])
        ctxn = sb("ctxn", [P, SLOTS, D])
        ctxT = sb("ctxT", [D, NT])
        lg = sb("lg", [P, SLOTS, EXPERTS])
        lgd = sb("lgd", [P, SLOTS, EXPERTS])
        lgt = sb("lgt", [P, SLOTS, EXPERTS])
        better = sb("better", [P, 3, SLOTS * EXPERTS, EXPERTS])
        erank = sb("erank", [P, SLOTS * EXPERTS])
        esel = sb("esel", [P, SLOTS, EXPERTS])
        esum = sb("esum", [P, 2, SLOTS])
        comb = sb("comb", [P, SLOTS, EXPERTS])
        combT = sb("combT", [EXPERTS, NT])
        part = sb("part", [P, 2, SLOTS, EXPERTS])
        comb3 = sb("comb3", [P, SLOTS, 3, EXPERTS], bf16)
        comb3T = sb("comb3T", [3 * EXPERTS, NT], bf16)
        ge = sb("ge", [P, 4, NT])
        gs = sb("gs", [P, 4, NT])

        psum = ctx.enter_context(nc.psum_tensor("psum", [P, 8, 512], fp32))
        B = [psum[:, i, :] for i in range(8)]

        in_ids, in_first, in_attn0, in_mid, in_moe = (sem(f"in_{n}") for n in ("ids", "first", "attn0", "mid", "moe"))
        in_x = [sem("in_x0"), sem("in_x1")]
        in_attr, out_done = sem("in_attr"), sem("out_done")
        s_warm, const_half, const_edge, const_l1, const_moe = (sem(n) for n in
                                                               ("warm_ready", "const_half", "const_edge", "const_l1", "const_moe"))
        s_posh, s_posh_ev, s_g, s_g_ev, s_bq = sem("posh_ps"), sem("posh_ready"), sem("g_ps"), sem("g_ready"), sem("bq_scaled")
        s_hot, s_expo, s_key, s_keyT = sem("onehot_ready"), sem("expo_ps"), sem("key_ready"), sem("keyT_ps")
        s_edge, s_attrT, s_attrT_ev = sem("edge_ready"), sem("attrT_ps"), sem("attrT_ready")
        s_eb, s_biasP, s_kb, s_kb_ev = sem("edgebias_ps"), sem("biasP_ready"), sem("kbias_ps"), sem("kbias_ready")
        s_emb, s_h0 = sem("emb_ps"), sem("h0_ready")
        s_h = sem("h_ready")
        s_st, s_mv, s_var, s_rstd = sem("stats_done"), sem("meanvar_done"), sem("var_ready"), sem("rstd_ready")
        s_xn, s_xt, s_xt_ev, s_res = sem("xn_ready"), sem("xT_ps"), sem("xT_ready"), sem("res_ready")
        s_q0, s_q0_ev, s_v0, s_v0_ev = sem("q0_ps"), sem("q0_ready"), sem("v0_ps"), sem("v0_ready")
        s_sc0, s_mx0, s_sub0, s_exp0 = sem("scores0_ps"), sem("max0_done"), sem("shifted0"), sem("exp0_done")
        s_sum0, s_rinv, s_wos, s_wosd = sem("sum0_done"), sem("rinv_ready"), sem("wos_ready"), sem("wos3_ready")
        s_m0, s_m0_ev, s_o0 = sem("mix0_ps"), sem("mix0_ready"), sem("attn0_ps")
        s_wr, s_hid, s_gelu, s_y = sem("weights_ps"), sem("hid_ps"), sem("gelu_ready"), sem("ffn_ps")
        s_vec = sem("vector_step")
        s_q1, s_q1_ev, s_k1, s_k1_ev = sem("q1_ps"), sem("q1_ready"), sem("k1_ps"), sem("k1_ready")
        s_v1, s_v1_ev, s_h2b = sem("v1_ps"), sem("v1_ready"), sem("h2_bias_ready")
        s_sc1, s_mx1, s_sub1, s_exp1 = sem("scores1_ps"), sem("max1_done"), sem("shifted1"), sem("exp1_done")
        s_et, s_et_ev_a, s_et_ev_v, s_av = sem("ET_ps"), sem("ET_ready_act"), sem("ET_ready_dve"), sem("ctx_ps")
        s_ctx, s_ctxT, s_ctxT_ev, s_o1 = sem("ctx_ready"), sem("ctxT_ps"), sem("ctxT_ready"), sem("attn1_ps")
        s_lg, s_lgd, s_lgt, s_comb = sem("logits_ps"), sem("logit_gap"), sem("logit_tanh"), sem("comb_ready")
        s_eh, s_eg, s_cr, s_gs = sem("expert_hid_ps"), sem("expert_gelu"), sem("comb_rep_ps"), sem("expert_scaled")
        s_ct, s_ct_ev, s_fin, s_out_v, s_out_a = sem("combT_ps"), sem("combT_ready"), sem("moe_ps"), sem("out_dve"), sem("out_act")

        s_c3, s_c3_ev = sem("comb3T_ps"), sem("comb3T_ready")
        C3 = B[3][0:3 * EXPERTS, 0:NT // 2].bitcast(bf16)

        block = ctx.enter_context(nc.Block())

        def bc(ap, axis, n):
            u = ap.unsqueeze(axis)
            shape = list(u.shape)
            shape[axis] = n
            return u.broadcast_to(shape)

        @block.sync
        def _(sp):
            def load(dst, src, s):
                sp.dma_start(dst, src).then_inc(s, 16)

            load(pack["first"][:, :], packs["first"], in_first)
            load(Xt[:, 0, 0:KX // 2, :], packs["x"][:, 0, 0:KX // 2, :], in_x[0])
            load(pack["attn0"][:, :], packs["attn0"], in_attn0)
            load(Xt[:, 1, 0:KX // 2, :], packs["x"][:, 1, 0:KX // 2, :], in_x[1])
            load(pack["mid"][:, :], packs["mid"], in_mid)
            load(pack["moe"][:, :], packs["moe"], in_moe)
            out_v = out.rearrange("(c s b) t d -> c (b t) s d", c=2, s=2)
            sp.wait_ge(s_out_v, 1)
            sp.dma_start(out_v[0], h[4][:, 0:2, :]).then_inc(out_done, 16)
            sp.wait_ge(s_out_a, 1)
            sp.dma_start(out_v[1], h[4][:, 2:4, :]).then_inc(out_done, 16)
            sp.wait_ge(out_done, 32)

        @block.gpsimd
        def _(pool):
            gp = nc.gpsimd
            gp.iota(iota16[:, :, :], [[1, 16], [0, P]], base=0, channel_multiplier=0,
                    allow_small_or_imprecise_dtypes=True).then_inc(const_edge, 1)
            gp.memset(neg_half[:, :], -0.5).then_inc(const_half, 1)
            pool.wait_ge(in_attn0, 16)
            gp.tensor_copy(row_pow[:, :], row_pow_f).then_inc(const_edge, 1)
            gp.tensor_copy(ident_h[:, :], ident).then_inc(const_moe, 1)
            gp.memset(biasP[:, :, :], 0.0).then_inc(const_l1, 1)
            gp.memset(attr[:, :], 1.0).then_inc(const_l1, 1)
            gp.memset(vB[:, :, :, :], 0.0).then_inc(const_l1, 1)
            pool.wait_ge(const_l1, 3)
            for u in range(2):
                gp.memset(vB[u * TOK:(u + 1) * TOK, :, :, u * (HD + 1) + HD:u * (HD + 1) + HD + 1], 1.0).then_inc(const_l1, 1)
                pool.wait_ge(const_l1, 4 + u)

            def power(k, c):
                n = 2 * k + c
                pool.wait_ge(s_var, n + 1)
                gp.tensor_tensor(rstd[:, k, 2 * c:2 * c + 2], var[:, k, 2 * c:2 * c + 2], neg_half[:, 0:2],
                                 ALU.pow).then_inc(s_rstd, 1)

            def residual(k, c):
                n = 2 * k + c
                pool.wait_ge(s_xn, n + 1)
                sl = slice(2 * c, 2 * c + 2)
                gp.tensor_tensor(res[k][:, sl, :], h[k][:, sl, :], xn[k][:, sl, 0, :], ALU.add).then_inc(s_res, 1)

            pool.wait_ge(const_half, 1)
            power(0, 0)
            power(0, 1)
            pool.wait_ge(s_edge, 1)
            gp.indirect_dma_start(out=attr[:, 0:3], out_offset=None, in_=I["L1_attn_edge_attr"],
                                  in_offset=bass.IndirectOffsetOnAxis(ap=edge_u[:, 0:1], axis=0)).then_inc(in_attr, 16)
            for s in range(SLOTS - 1):
                pool.wait_ge(s_rinv, s + 1)
                for u in range(2):
                    gp.tensor_tensor(WoS[:, s, 4 * u:4 * u + 4, :].rearrange("p (b n) d -> p b n d", b=2),
                                     bc(WoT[:, 2 * u:2 * u + 2, :], 1, 2),
                                     bc(top0[:, 2, s, 4 * u:4 * u + 4].rearrange("p (b n) -> p b n", b=2), 3, D),
                                     ALU.mult).then_inc(s_wos, 1)
            power(1, 0)
            power(1, 1)
            pool.wait_ge(in_moe, 16)
            gp.tensor_copy(sel3[:, :, :].rearrange("k q m -> k (q m)"), at["sel3"]).then_inc(const_moe, 1)
            residual(1, 0)
            residual(1, 1)
            power(2, 0)
            power(2, 1)
            for c in range(2):
                sl = slice(2 * c, 2 * c + 2)
                gp.tensor_tensor(res[2][:, sl, :], h[2][:, sl, :], bc(bo_rep, 1, 2), ALU.add).then_inc(s_h2b, 1)
            power(3, 0)
            power(3, 1)
            residual(3, 0)
            residual(3, 1)

        @block.scalar
        def _(act):
            sc = nc.scalar
            act.dma_start(ids[:, :], I["L1_attn_edge_index"][1, :].rearrange("(p e) -> p e", p=P)).then_inc(in_ids, 16)
            for c in range(2):
                act.dma_start(Xt[:, c, KX // 2:KX, :], packs["x"][:, c, KX // 2:KX, :]).then_inc(in_x[c], 16)

            def layer_xT(k, c):
                n = 2 * k + c
                rows_ = P if k == 0 else D
                act.wait_ge(s_xt, n + 1)
                sc.activation(xT[k][0:rows_, c * HALF:(c + 1) * HALF], B[c][0:rows_, 0:HALF], ACT.Copy).then_inc(s_xt_ev, 1)

            act.wait_ge(s_posh, 1)
            sc.activation(posh[0:D, :], B[4][0:D, 0:P], ACT.Relu).then_inc(s_posh_ev, 1)
            for c in range(2):
                act.wait_ge(s_emb, c + 1)
                sc.activation(h[0][:, 2 * c:2 * c + 2, :].rearrange("p s d -> p (s d)"), B[2 + c][:, 0:P],
                              ACT.Copy).then_inc(s_h0, 1)
                if c == 0:
                    act.wait_ge(s_g, 1)
                    sc.activation(G[:, 0:HEADS:2, :], B[6][0:D, 0:256].rearrange("p (q c) -> p q c", c=D), ACT.Copy).then_inc(s_g_ev, 1)
                    sc.activation(G[:, 1:HEADS:2, :], B[5][0:D, 0:256].rearrange("p (q c) -> p q c", c=D), ACT.Copy).then_inc(s_g_ev, 1)
            for c in range(2):
                layer_xT(0, c)
                for u in range(2):
                    act.wait_ge(s_q0, 2 * c + u + 1)
                    bank = (B[4], B[5], B[6], B[2])[2 * c + u]
                    sc.activation(qT0[:, u, 4 * c:4 * c + 4, :, :].rearrange("p b q n -> p q b n"),
                                  bank[:, :].rearrange("p (q b n) -> p q b n", q=2, n=TOK), ACT.Copy).then_inc(s_q0_ev, 1)
            act.wait_ge(s_v0, 1)
            sc.activation(v0[:, :], B[3][:, :], ACT.Copy).then_inc(s_v0_ev, 1)
            for s in range(SLOTS):
                act.wait_ge(s_sub0, s + 1)
                sc.activation(E0[:, s, :, :], E0[:, s, :, :], ACT.Exp, scale=SC0).then_inc(s_exp0, 1)
            sc.preload_act_table(ACT.Gelu_apprx_tanh)
            act.wait_ge(in_mid, 16)
            sc.activation(bq_scaled[:, :], bq1, ACT.Copy, scale=SC0).then_inc(s_bq, 1)
            for c in range(2):
                act.wait_ge(s_m0, c + 1)
                bank = (B[6], B[2])[c]
                sc.activation(M0[:, 2 * c:2 * c + 2, :].rearrange("p s d -> p (s d)"), bank[:, 0:P], ACT.Copy).then_inc(s_m0_ev, 1)
            layer_xT(1, 0)
            layer_xT(1, 1)
            for c in range(2):
                act.wait_ge(s_hid, c + 1)
                for k in range(2):
                    sc.activation(hid[:, k, c * HALF:(c + 1) * HALF], B[4 + c][:, k * HALF:(k + 1) * HALF],
                                  ACT.Gelu_apprx_tanh, bias=b1f[:, k:k + 1]).then_inc(s_gelu, 1)
            sc.preload_act_table(ACT.Exp)
            layer_xT(2, 0)
            layer_xT(2, 1)
            act.wait_ge(s_bq, 1)
            for c in range(2):
                act.wait_ge(s_q1, c + 1)
                for g in range(2):
                    sc.activation(qT1[:, g, c * HALF:(c + 1) * HALF], B[4 + 2 * c][:, g * HALF:(g + 1) * HALF],
                                  ACT.Identity, bias=bq_scaled[:, g:g + 1], scale=SC0).then_inc(s_q1_ev, 1)

            def exp1(s):
                act.wait_ge(s_sub1, s + 1)
                sc.activation(E1[:, s, :, :], E1[:, s, :, :], ACT.Exp).then_inc(s_exp1, 1)

            def et_copy(s):
                act.wait_ge(s_et, s + 1)
                bank = B[(1, 2, 3, 6)[s]]
                sc.activation(ET[:, s, :, :].rearrange("p q n -> p (q n)"), bank[:, :], ACT.Copy).then_inc(s_et_ev_a, 1)

            exp1(0)
            exp1(1)
            et_copy(0)
            et_copy(1)
            exp1(2)
            exp1(3)
            et_copy(2)
            sc.preload_act_table(ACT.Gelu)
            for c in range(2):
                act.wait_ge(s_ctxT, c + 1)
                bank = (B[7], B[0])[c]
                sc.activation(ctxT[:, c * HALF:(c + 1) * HALF], bank[0:D, 0:HALF], ACT.Copy).then_inc(s_ctxT_ev, 1)
            layer_xT(3, 0)
            layer_xT(3, 1)
            act.wait_ge(in_moe, 16)
            for q in range(4):
                if q == 2:
                    act.wait_ge(s_lgd, 1)
                    sc.activation(lgt[:, :, :], lgd[:, :, :], ACT.Tanh).then_inc(s_lgt, 1)
                act.wait_ge(s_eh, q + 1)
                sc.activation(ge[:, q, :], B[4 + q][:, :], ACT.Gelu, bias=b1e[:, q:q + 1]).then_inc(s_eg, 1)
            act.wait_ge(s_ct, 1)
            sc.activation(combT[:, :], B[4][0:EXPERTS, :], ACT.Copy).then_inc(s_ct_ev, 1)
            act.wait_ge(s_fin, 1)
            act.wait_ge(s_out_v, 1)
            sc.activation(h[4][:, 2:4, :].rearrange("p s d -> p (s d)"), B[5][:, P:2 * P], ACT.Copy).then_inc(s_out_a, 1)

        @block.vector
        def _(dve):
            ve = nc.vector
            step = [0]

            def link(ins):
                step[0] += 1
                ins.then_inc(s_vec, 1)
                dve.wait_ge(s_vec, step[0])

            ve.memset(warm[:, :], 0.0).then_inc(s_warm, 1)
            ve.memset(posh[D:D + 2, :], 1.0).then_inc(s_warm, 1)
            dve.wait_ge(in_ids, 16)
            link(ve.tensor_scalar(idf[:, 0, :], ids[:, :], 0.0, float(TOK), ALU.is_lt, ALU.mult))
            link(ve.tensor_tensor(idf[:, 1, :], ids[:, :], idf[:, 0, :], ALU.add))
            link(ve.tensor_scalar(idf[:, 2, :], idf[:, 1, :], float(TOK), -1.0, ALU.min, ALU.max))
            for k in range(4):
                ins = ve.tensor_scalar(idb[:, k, :], idf[:, 2, :], float(-16 * k), None, ALU.add)
            link(ins)
            dve.wait_ge(const_edge, 1)
            for k in range(4):
                ve.tensor_tensor(onehot[:, 16 * k:16 * k + 16, :], bc(idb[:, k, :], 1, 16), iota16[:, :, :],
                                 ALU.is_equal).then_inc(s_hot, 1)

            def ln_stats(k, c):
                for s in (2 * c, 2 * c + 1):
                    ve.bn_stats(stats[:, k, s, :], h[k][:, s, :]).then_inc(s_st, 1)
                for s in (2 * c, 2 * c + 1):
                    dve.wait_ge(s_st, 4 * k + s + 1)
                    ve.bn_aggr(mv[:, k, s, :], stats[:, k, s, :]).then_inc(s_mv, 1)
                dve.wait_ge(s_mv, 4 * k + 2 * c + 2)
                ve.tensor_scalar(var[:, k, 2 * c:2 * c + 2], mv[:, k, 2 * c:2 * c + 2, 1], EPS, None,
                                 ALU.add).then_inc(s_var, 1)

            def ln_norm(k, c):
                dve.wait_ge(s_rstd, 2 * k + c + 1)
                for s in (2 * c, 2 * c + 1):
                    copies = 2 if k == 0 else 1
                    ins = ve.tensor_scalar(xn[k][:, s, 0:copies, :], bc(h[k][:, s, :], 1, copies), mv[:, k, s, 0:1],
                                           rstd[:, k, s:s + 1], ALU.subtract, ALU.mult)
                ins.then_inc(s_xn, 1)

            for c in range(2):
                dve.wait_ge(s_h0, c + 1)
                ln_stats(0, c)
                ln_norm(0, c)

            dve.wait_ge(s_expo, 4)
            dve.wait_ge(in_attn0, 16)
            link(ve.tensor_scalar(expo[:, :, :], B[7][:, 0:2 * TOK].bitcast(i32).rearrange("p (j u) -> p j u", u=2),
                                  23, None, ALU.logical_shift_right))
            link(ve.tensor_scalar(last[:, 0, :], expo[:, :, 1], 0.0, 128.0, ALU.is_gt, ALU.mult))
            link(ve.tensor_tensor(last[:, 1, :], last[:, 0, :], expo[:, :, 1], ALU.add))
            link(ve.tensor_tensor(last[:, 2, :], last[:, 1, :], expo[:, :, 0], ALU.max))
            ve.tensor_scalar(last[:, 0, :], last[:, 2, :], float(D), col_idx, ALU.mult, ALU.add).then_inc(s_key, 1)

            def softmax0_shift(s):
                c, j = s // 2, s % 2
                S = psum[:, 4 * c:4 * c + 2, j * 256:(j + 1) * 256].rearrange("p u (q t) -> p u q t", t=TOK)
                top = top0[:, 0, s, :].rearrange("p (u q) -> p u q", u=2)
                dve.wait_ge(s_sc0, c + 1)
                ve.tensor_reduce(top, S, X, ALU.max).then_inc(s_mx0, 1)
                dve.wait_ge(s_mx0, s + 1)
                ve.tensor_tensor(E0[:, s, :, :].rearrange("p (u q) t -> p u q t", u=2), S, bc(top, 3, TOK),
                                 ALU.subtract).then_inc(s_sub0, 1)

            def softmax0_sum(s):
                dve.wait_ge(s_exp0, s + 1)
                ve.tensor_reduce(top0[:, 1, s, :], E0[:, s, :, :], X, ALU.add).then_inc(s_sum0, 1)
                dve.wait_ge(s_sum0, s + 1)
                ve.reciprocal(top0[:, 2, s, :], top0[:, 1, s, :]).then_inc(s_rinv, 1)

            softmax0_shift(0)
            softmax0_shift(1)
            softmax0_sum(0)
            softmax0_sum(1)
            dve.wait_ge(s_keyT, 1)
            link(ve.tensor_reduce(edge[:, 0:1], B[7][0:TOK, 256:256 + P], X, ALU.max))
            link(ve.tensor_scalar(edge[:, 1:2], edge[:, 0:1], float(ABSENT), None, ALU.is_ge))
            link(ve.tensor_scalar(edge_u[:, 0:1], edge[:, 0:1], float(-ABSENT), 0.0, ALU.add, ALU.max))
            dve.sem_inc(s_edge, 1)
            softmax0_shift(2)
            softmax0_shift(3)
            softmax0_sum(2)
            softmax0_sum(3)
            dve.wait_ge(s_rinv, 4)
            for u in range(2):
                ve.tensor_tensor(WoS[:, 3, 4 * u:4 * u + 4, :].rearrange("p (b n) d -> p b n d", b=2),
                                 bc(WoT[:, 2 * u:2 * u + 2, :], 1, 2),
                                 bc(top0[:, 2, 3, 4 * u:4 * u + 4].rearrange("p (b n) -> p b n", b=2), 3, D),
                                 ALU.mult).then_inc(s_wosd, 1)
            for c in range(2):
                dve.wait_ge(s_o0, c + 1)
                sl = slice(2 * c, 2 * c + 2)
                ve.tensor_tensor(h[1][:, sl, :], h[0][:, sl, :], (B[3], B[7])[c][:, 0:P].rearrange("p (s d) -> p s d", s=2),
                                 ALU.add).then_inc(s_h, 1)
                dve.wait_ge(s_h, c + 1)
                ln_stats(1, c)
            ln_norm(1, 0)
            ln_norm(1, 1)
            dve.wait_ge(s_attrT, 1)
            ve.tensor_copy(attrT[:, :], B[7][0:4, 256:256 + TOK]).then_inc(s_attrT_ev, 1)

            dve.wait_ge(s_wr, 1)
            dve.wait_ge(in_mid, 16)
            link(ve.tensor_scalar(wall[:, :, :].rearrange("p s n -> p (s n)"), B[6][:, 0:256], br, None, ALU.add))
            link(ve.tensor_tensor(wdiag[:, :, :], wall[:, :, :], bc(eye2, 1, SLOTS), ALU.mult))
            link(ve.tensor_reduce(wcol[:, :], wdiag[:, :, :], X, ALU.add))
            for s in range(SLOTS):
                ins = ve.scalar_tensor_tensor(tie[:, s, :], wall[:, s, :], wcol[:, s:s + 1], earlier,
                                              ALU.is_equal, ALU.mult)
            link(ins)
            for s in range(SLOTS):
                ins = ve.scalar_tensor_tensor(ahead[:, s, :], wall[:, s, :], wcol[:, s:s + 1], tie[:, s, :],
                                              ALU.is_gt, ALU.add, accum_out=rank[:, s:s + 1])
            link(ins)
            link(ve.scalar_tensor_tensor(gate[:, :], rank[:, :], float(KSEL), wcol[:, :], ALU.is_lt, ALU.mult))
            dve.wait_ge(s_eb, 1)
            dve.wait_ge(const_l1, 1)
            ve.tensor_scalar(biasP[:, :, :].rearrange("j g (h k) -> j g h k", h=4)[:, :, :, HD:HD + 1].rearrange("j g h k -> j g (h k)"),
                             B[7][0:TOK, 448:456].rearrange("j (g h) -> j g h", g=2), edge[:, 1:2], None, ALU.mult).then_inc(s_biasP, 1)
            for c in range(2):
                dve.wait_ge(s_y, c + 1)
                dve.wait_ge(s_res, c + 1)
                for j in range(2):
                    s = 2 * c + j
                    ins = ve.scalar_tensor_tensor(h[2][:, s, :], (B[2], B[3])[c][:, j * D:(j + 1) * D], gate[:, s:s + 1],
                                                  res[1][:, s, :], ALU.mult, ALU.add)
                ins.then_inc(s_h, 1)
                dve.wait_ge(s_h, 2 + c + 1)
                ln_stats(2, c)
            ln_norm(2, 0)
            ln_norm(2, 1)
            dve.wait_ge(s_kb, 1)
            for g in range(2):
                ins = ve.tensor_scalar(kbias[:, g, :], B[7][:, 320 + g * TOK:320 + (g + 1) * TOK], bk1[:, g:g + 1],
                                       None, ALU.add)
            ins.then_inc(s_kb_ev, 1)
            dve.wait_ge(s_kb_ev, 1)
            for c in range(2):
                dve.wait_ge(s_k1, c + 1)
                for g in range(2):
                    ve.tensor_tensor(kT1[:, g, c * HALF:(c + 1) * HALF].rearrange("p (b n) -> p b n", n=TOK),
                                     B[5 + 2 * c][:, g * HALF:(g + 1) * HALF].rearrange("p (b n) -> p b n", n=TOK),
                                     bc(kbias[:, g, :], 1, 4), ALU.add).then_inc(s_k1_ev, 1)
            dve.wait_ge(const_l1, 5)

            def softmax1_shift(s):
                c, j = s // 2, s % 2
                S = psum[:, 4 * c:4 * c + 4, j * P:(j + 1) * P].rearrange("p q (g t) -> p q g t", t=TOK)
                top = top1[:, s, :].rearrange("p (q g) -> p q g", g=2)
                dve.wait_ge(s_sc1, c + 1)
                ve.tensor_reduce(top, S, X, ALU.max).then_inc(s_mx1, 1)
                dve.wait_ge(s_mx1, s + 1)
                ve.tensor_tensor(E1[:, s, :, :].rearrange("p (q g) t -> p q g t", g=2), S, bc(top, 3, TOK),
                                 ALU.subtract).then_inc(s_sub1, 1)

            for s in range(SLOTS):
                softmax1_shift(s)
            dve.wait_ge(s_v1, 1)
            for u in range(2):
                half = slice(u * TOK, (u + 1) * TOK)
                ins = ve.tensor_tensor(vB[half, :, :, u * (HD + 1):u * (HD + 1) + HD],
                                       B[0][half, :].rearrange("p (b q k) -> p b q k", b=BATCH, k=HD)[:, :, 4 * u:4 * u + 4, :],
                                       bc(bv_rep[half, :].rearrange("p (q k) -> p q k", k=HD)[:, 4 * u:4 * u + 4, :], 1, BATCH),
                                       ALU.add)
            ins.then_inc(s_v1_ev, 1)
            dve.wait_ge(s_et, 4)
            ve.tensor_copy(ET[:, 3, :, :].rearrange("p q n -> p (q n)"), B[6][:, :]).then_inc(s_et_ev_v, 1)
            for c in range(2):
                sl = slice(2 * c, 2 * c + 2)
                C = (B[4], B[5])[c][:, 0:2 * HEADS * (HD + 1)].rearrange("p (s q k) -> p s q k", s=2, k=HD + 1)
                dve.wait_ge(s_av, c + 1)
                link(ve.reciprocal(rden[:, sl, :], C[:, :, :, HD]))
                for g in range(2):
                    ins = ve.tensor_tensor(ctxn[:, sl, 32 * g:32 * g + 32].rearrange("p s (q k) -> p s q k", k=HD),
                                           C[:, :, g:HEADS:2, 0:HD], bc(rden[:, sl, g:HEADS:2], 3, HD), ALU.mult)
                ins.then_inc(s_ctx, 1)
            for c in range(2):
                sl = slice(2 * c, 2 * c + 2)
                dve.wait_ge(s_o1, c + 1)
                dve.wait_ge(s_h2b, c + 1)
                ve.tensor_tensor(h[3][:, sl, :], res[2][:, sl, :], (B[1], B[2])[c][:, 0:P].rearrange("p (s d) -> p s d", s=2),
                                 ALU.add).then_inc(s_h, 1)
                dve.wait_ge(s_h, 4 + c + 1)
                ln_stats(3, c)
            ln_norm(3, 0)
            ln_norm(3, 1)

            dve.wait_ge(s_lg, 1)
            link(ve.tensor_copy(lg[:, :, :].rearrange("p s e -> p (s e)"), B[3][:, 0:SLOTS * EXPERTS]))
            dve.wait_ge(in_moe, 16)
            other = bc(lg[:, :, :], 2, EXPERTS)
            own = bc(lg[:, :, :], 3, EXPERTS)
            bt = [better[:, n, :, :].rearrange("p (s e) f -> p s e f", e=EXPERTS) for n in range(3)]
            link(ve.tensor_tensor(bt[0], other, own, ALU.is_equal))
            link(ve.tensor_tensor(bt[1], bt[0], bc(earlier8, 1, SLOTS), ALU.mult))
            link(ve.tensor_tensor(bt[2], other, own, ALU.is_gt))
            link(ve.tensor_tensor(bt[0], bt[1], bt[2], ALU.add))
            link(ve.tensor_reduce(erank[:, :], better[:, 0, :, :], X, ALU.add))
            lgs = lg[:, :, :].rearrange("p s e -> p (s e)")
            sel = esel[:, :, :].rearrange("p s e -> p (s e)")
            link(ve.scalar_tensor_tensor(sel, erank[:, :], 2.0, lgs, ALU.is_lt, ALU.mult))
            link(ve.tensor_reduce(esum[:, 0, :], esel[:, :, :], X, ALU.add))
            link(ve.tensor_scalar(esum[:, 1, :], esum[:, 0, :], 0.5, None, ALU.mult))
            ve.tensor_tensor(lgd[:, :, :], lg[:, :, :], bc(esum[:, 1, :], 2, EXPERTS), ALU.subtract).then_inc(s_lgd, 1)
            dve.wait_ge(s_lgt, 1)
            link(ve.tensor_scalar(sel, lgt[:, :, :].rearrange("p s e -> p (s e)"), 0.5, 0.5, ALU.mult, ALU.add))
            ve.scalar_tensor_tensor(comb[:, :, :].rearrange("p s e -> p (s e)"), erank[:, :], 2.0, sel,
                                    ALU.is_lt, ALU.mult).then_inc(s_comb, 1)
            dve.wait_ge(s_comb, 1)
            link(ve.tensor_copy(comb3[:, :, 0, :], comb[:, :, :]))
            link(ve.tensor_tensor(part[:, 0, :, :], comb[:, :, :], comb3[:, :, 0, :], ALU.subtract))
            link(ve.tensor_copy(comb3[:, :, 1, :], part[:, 0, :, :]))
            link(ve.tensor_tensor(part[:, 1, :, :], part[:, 0, :, :], comb3[:, :, 1, :], ALU.subtract))
            ve.tensor_copy(comb3[:, :, 2, :], part[:, 1, :, :]).then_inc(s_comb, 1)
            dve.wait_ge(s_c3, 1)
            ve.tensor_copy(comb3T[:, :], C3[:, :]).then_inc(s_c3_ev, 1)
            for q in range(4):
                dve.wait_ge(s_eg, q + 1)
                dve.wait_ge(s_cr, q + 1)
                ve.tensor_tensor(gs[:, q, :], ge[:, q, :], (B[2], B[1], B[0], B[3])[q][:, :], ALU.mult).then_inc(s_gs, 1)
            dve.wait_ge(s_fin, 1)
            ve.tensor_copy(h[4][:, 0:2, :].rearrange("p s d -> p (s d)"), B[5][:, 0:P]).then_inc(s_out_v, 1)

        @block.tensor
        def _(pe):
            mm = nc.tensor.matmul

            def tr(o, i, n):
                return nc.tensor.transpose(o, i, ident[0:n, 0:n])

            def keep_clock(bank, n):
                for _ in range(n):
                    mm(B[bank][:, :], lhsT=warm[:, 0:P], rhs=warm[:, :], start=True, stop=True)

            pe.wait_ge(s_warm, 1)
            keep_clock(0, WARM)
            pe.wait_ge(in_first, 16)
            mm(B[4][0:D, 0:P], lhsT=posW1, rhs=grid, start=True, stop=True).then_inc(s_posh, 1)

            def embed(c):
                pe.wait_ge(in_x[c], 32)
                for j in range(2):
                    o = B[2 + c][:, j * D:(j + 1) * D]
                    for q in range(KX):
                        mm(o, lhsT=Xt[:, c, q, j * P:(j + 1) * P], rhs=Wp[:, q, :], start=(q == 0), stop=False)
                    if c == 0 and j == 0:
                        pe.wait_ge(s_posh_ev, 1)
                        pe.wait_ge(s_warm, 2)
                    ins = mm(o, lhsT=posh[:, :], rhs=posW2, start=False, stop=True)
                ins.then_inc(s_emb, 1)

            def last_rows(k):
                pe.wait_ge(s_hot, k + 1)
                pe.wait_ge(const_edge, 2)
                for j in range(16 * k, 16 * k + 16):
                    ins = mm(B[7][:, 2 * j:2 * j + 2], lhsT=onehot[:, j, :], rhs=row_pow[:, :], start=True, stop=True)
                ins.then_inc(s_expo, 1)

            def layer_xT(k, c):
                pe.wait_ge(s_xn, 2 * k + c + 1)
                for j in range(2):
                    s = 2 * c + j
                    if k == 0:
                        ins = tr(B[c][:, j * P:(j + 1) * P], xn[k][:, s, :, :], P)
                    else:
                        ins = tr(B[c][0:D, j * P:(j + 1) * P], xn[k][:, s, 0, :], P)
                ins.then_inc(s_xt, 1)

            embed(0)
            pe.wait_ge(in_attn0, 16)
            for k in range(4):
                mm(B[6][0:D, k * D:(k + 1) * D], lhsT=Wq0[0:D, k, :], rhs=Wk0[0:D, :], start=True, stop=True)
                ins = mm(B[5][0:D, k * D:(k + 1) * D], lhsT=Wq0[D:P, k, :], rhs=Wk0[D:P, :], start=True, stop=True)
            ins.then_inc(s_g, 1)
            embed(1)
            keep_clock(1, 6)
            layer_xT(0, 0)

            def queries0(c):
                pe.wait_ge(s_xt_ev, c + 1)
                for u in range(2):
                    if c == 0 and u == 0:
                        pe.wait_ge(s_g_ev, 2)
                    if c == 1 and u == 0:
                        pe.wait_ge(s_h0, 2)
                    bank = (B[4], B[5], B[6], B[2])[2 * c + u]
                    for q in range(2):
                        ins = mm(bank[:, q * HALF:(q + 1) * HALF], lhsT=G[:, 4 * u + 2 * q:4 * u + 2 * q + 2, :],
                                 rhs=xT[0][0:D, c * HALF:(c + 1) * HALF], start=True, stop=True)
                    ins.then_inc(s_q0, 1)

            def scores0(c):
                pe.wait_ge(s_q0_ev, 2 * c + 2)
                for j in range(2):
                    for b in range(2):
                        keep_clock((4, 6)[c], 1)
                        tok = c * HALF + j * P + b * TOK
                        for n in range(2):
                            for par in range(2):
                                q = 4 * j + 2 * b + n
                                ins = mm(B[4 * c + par][:, q * TOK:(q + 1) * TOK],
                                         lhsT=qT0[par * D:(par + 1) * D, n, 4 * c + 2 * j + b, :, :],
                                         rhs=xT[0][par * D:(par + 1) * D, tok:tok + TOK], start=True, stop=True)
                ins.then_inc(s_sc0, 1)

            keep_clock(1, 6)
            for k in range(4):
                last_rows(k)
                keep_clock(1, 2)
            queries0(0)
            layer_xT(0, 1)
            pe.wait_ge(s_xt_ev, 2)
            scores0(0)
            queries0(1)
            mm(B[3][:, :], lhsT=WvT, rhs=xT[0][0:D, :], start=True, stop=True).then_inc(s_v0, 1)
            pe.wait_ge(s_key, 1)
            tr(B[7][0:TOK, 256:256 + P], last[:, 0, :], P).then_inc(s_keyT, 1)
            scores0(1)
            pe.wait_ge(s_q0_ev, 4)
            keep_clock(6, 6)
            for c in range(2):
                bank = (B[6], B[2])[c]
                for j in range(2):
                    s = 2 * c + j
                    pe.wait_ge(s_exp0, s + 1)
                    if s < 3:
                        pe.wait_ge(s_wos, 2 * s + 2)
                    else:
                        pe.wait_ge(s_wosd, 2)
                    if s == 0:
                        pe.wait_ge(s_q0_ev, 4)
                    for q in range(4):
                        for b in range(2):
                            ins = mm(bank[b * D:(b + 1) * D, j * D:(j + 1) * D], lhsT=E0[:, s, 4 * (q // 2) + 2 * b + q % 2, :],
                                     rhs=WoS[:, s, 4 * (q // 2) + 2 * b + q % 2, :], start=(q == 0), stop=(q == 3))
                ins.then_inc(s_m0, 1)
                pe.wait_ge(s_m0_ev, c + 1)
                pe.wait_ge(s_v0_ev, 1)
                if c == 1:
                    pe.wait_ge(s_edge, 1)
                for b in range(2):
                    for j in range(2):
                        tok = c * HALF + j * P + b * TOK
                        ins = mm((B[3], B[7])[c][b * D:(b + 1) * D, j * D:(j + 1) * D], lhsT=v0[b * D:(b + 1) * D, tok:tok + TOK],
                                 rhs=M0[b * D:(b + 1) * D, 2 * c + j, :], start=True, stop=True)
                ins.then_inc(s_o0, 1)

            pe.wait_ge(in_mid, 16)
            keep_clock(0, 6)
            layer_xT(1, 0)
            layer_xT(1, 1)
            pe.wait_ge(s_h, 2)
            pe.wait_ge(in_attr, 16)
            tr(B[7][0:4, 256:256 + TOK], attr[:, :], TOK).then_inc(s_attrT, 1)
            for c in range(2):
                pe.wait_ge(s_xt_ev, 2 + c + 1)
                for k in range(2):
                    ins = mm(B[4 + c][:, k * HALF:(k + 1) * HALF], lhsT=w1f[:, k * P:(k + 1) * P],
                             rhs=xT[1][0:D, c * HALF:(c + 1) * HALF], start=True, stop=True)
                ins.then_inc(s_hid, 1)
            for b in range(2):
                rhs = xT[1][0:D, :].rearrange("d (s b n) -> d s b n", b=2, n=TOK)[:, :, b, :]
                ins = mm(B[6][b * D:(b + 1) * D, 0:256], lhsT=wr.broadcast_to([D, D]), rhs=rhs, start=True, stop=True)
            ins.then_inc(s_wr, 1)
            pe.wait_ge(s_attrT_ev, 1)
            mm(B[7][0:TOK, 448:456], lhsT=attrT[:, :], rhs=WeB, start=True, stop=True).then_inc(s_eb, 1)
            for c in range(2):
                pe.wait_ge(s_gelu, 2 * c + 2)
                for j in range(2):
                    s = 2 * c + j
                    o = (B[2], B[3])[c][:, j * D:(j + 1) * D]
                    for k in range(2):
                        mm(o, lhsT=hid[:, k, s * P:(s + 1) * P], rhs=w2f[:, k, :], start=(k == 0), stop=False)
                    ins = mm(o, lhsT=ones_row, rhs=b2f, start=False, stop=True)
                ins.then_inc(s_y, 1)
            pe.wait_ge(s_biasP, 1)
            for g in range(2):
                ins = mm(B[7][:, 320 + g * TOK:320 + (g + 1) * TOK], lhsT=biasP[:, g, :], rhs=ident[0:TOK, 0:TOK],
                         start=True, stop=True)
            ins.then_inc(s_kb, 1)

            keep_clock(0, 8)
            layer_xT(2, 0)
            layer_xT(2, 1)
            for c in range(2):
                pe.wait_ge(s_xt_ev, 4 + c + 1)
                src = xT[2][0:D, c * HALF:(c + 1) * HALF]
                for g in range(2):
                    ins = mm(B[4 + 2 * c][:, g * HALF:(g + 1) * HALF], lhsT=WqP[:, g, :], rhs=src, start=True, stop=True)
                ins.then_inc(s_q1, 1)
                if c == 1:
                    pe.wait_ge(s_kb_ev, 1)
                for g in range(2):
                    ins = mm(B[5 + 2 * c][:, g * HALF:(g + 1) * HALF], lhsT=WkP[:, g, :], rhs=src, start=True, stop=True)
                ins.then_inc(s_k1, 1)

            def scores1(c):
                pe.wait_ge(s_q1_ev, 2 * c + 2 if c == 0 else 4)
                pe.wait_ge(s_k1_ev, 2 * c + 2)
                for j in range(2):
                    for g in range(2):
                        if c == 0:
                            keep_clock(4, 3)
                        col = (2 * j + g) * TOK
                        for hh in range(4):
                            rows_ = slice(32 * hh, 32 * hh + HD + 1)
                            for b in range(2):
                                tok = c * HALF + j * P + b * TOK
                                ins = mm(B[4 * c + hh][b * D:(b + 1) * D, col:col + TOK], lhsT=qT1[rows_, g, tok:tok + TOK],
                                         rhs=kT1[rows_, g, tok:tok + TOK], start=True, stop=True)
                ins.then_inc(s_sc1, 1)

            def values1():
                pe.wait_ge(s_sub1, 2)
                for b in range(BATCH):
                    for u in range(2):
                        ins = mm(B[0][u * D:(u + 1) * D, b * D:(b + 1) * D], lhsT=xT[2][0:D, b * TOK:(b + 1) * TOK],
                                 rhs=Wv1, start=True, stop=True)
                ins.then_inc(s_v1, 1)

            def probsT(s):
                pe.wait_ge(s_exp1, s + 1)
                bank = B[(1, 2, 3, 6)[s]]
                for q in range(4):
                    ins = tr(bank[:, q * P:(q + 1) * P], E1[:, s, 2 * q:2 * q + 2, :], P)
                ins.then_inc(s_et, 1)

            def context(c):
                for j in range(2):
                    s = 2 * c + j
                    if s < 3:
                        pe.wait_ge(s_et_ev_a, s + 1)
                    else:
                        pe.wait_ge(s_et_ev_v, 1)
                    for q in range(4):
                        for b in range(2):
                            col = (j * 4 + q) * 2 * (HD + 1)
                            ins = mm((B[4], B[5])[c][b * D:(b + 1) * D, col:col + 2 * (HD + 1)],
                                     lhsT=ET[:, s, q, b * TOK:(b + 1) * TOK], rhs=vB[:, 2 * s + b, q, :], start=True, stop=True)
                ins.then_inc(s_av, 1)

            scores1(0)
            scores1(1)
            values1()
            probsT(0)
            probsT(1)
            probsT(2)
            pe.wait_ge(s_v1_ev, 1)
            pe.wait_ge(s_sub1, 4)
            context(0)
            probsT(3)
            context(1)
            for c in range(2):
                pe.wait_ge(s_ctx, c + 1)
                for j in range(2):
                    ins = tr((B[7], B[0])[c][0:D, j * P:(j + 1) * P], ctxn[:, 2 * c + j, :], P)
                ins.then_inc(s_ctxT, 1)
            for c in range(2):
                pe.wait_ge(s_ctxT_ev, c + 1)
                for j in range(2):
                    s = 2 * c + j
                    ins = mm((B[1], B[2])[c][:, j * D:(j + 1) * D], lhsT=ctxT[:, s * P:(s + 1) * P], rhs=Wo1,
                             start=True, stop=True)
                ins.then_inc(s_o1, 1)

            pe.wait_ge(s_ctxT_ev, 2)
            keep_clock(0, 6)
            layer_xT(3, 0)
            layer_xT(3, 1)
            pe.wait_ge(in_moe, 16)
            pe.wait_ge(s_xt_ev, 8)
            for s in range(SLOTS):
                ins = mm(B[3][:, s * EXPERTS:(s + 1) * EXPERTS], lhsT=xT[3][0:D, s * P:(s + 1) * P], rhs=rwT,
                         start=True, stop=True)
            ins.then_inc(s_lg, 1)
            for q in range(4):
                mm(B[4 + q][:, :], lhsT=w1e[:, 2 * q:2 * q + 2, :], rhs=xT[3][0:D, :], start=True, stop=True).then_inc(s_eh, 1)
            keep_clock(2, 6)
            pe.wait_ge(s_comb, 2)
            pe.wait_ge(const_moe, 2)
            for s in range(SLOTS):
                ins = nc.tensor.transpose(C3[:, s * P:(s + 1) * P], comb3[:, s, :, :], ident_h[:, :])
            ins.then_inc(s_c3, 1)
            pe.wait_ge(s_c3_ev, 1)
            for q in range(4):
                mm((B[2], B[1], B[0], B[3])[q][:, :], lhsT=sel3[:, q, :], rhs=comb3T[:, :], start=True, stop=True).then_inc(s_cr, 1)
            pe.wait_ge(s_eg, 1)
            for s in range(SLOTS):
                ins = tr(B[4][0:EXPERTS, s * P:(s + 1) * P], comb[:, s, :], P)
            ins.then_inc(s_ct, 1)
            pe.wait_ge(s_eg, 2)
            pe.wait_ge(s_res, 4)
            F = B[5]
            mm(F[:, 0:256], lhsT=ident, rhs=res[3][:, :, :].rearrange("p s d -> p (s d)"), start=True, stop=True)
            pe.wait_ge(s_ct_ev, 1)
            for s in range(SLOTS):
                mm(F[:, s * D:(s + 1) * D], lhsT=combT[:, s * P:(s + 1) * P], rhs=b2e, start=False, stop=False,
                   skip_group_check=True)
            for q in range(4):
                pe.wait_ge(s_gs, q + 1)
                for s in range(SLOTS):
                    ins = mm(F[:, s * D:(s + 1) * D], lhsT=gs[:, q, s * P:(s + 1) * P], rhs=w2e[:, q, :], start=False,
                             stop=(q == 3), skip_group_check=True)
            ins.then_inc(s_fin, 1)


_OUTS = [((8, 64, 64), 'float32')]


def kernel(**inputs):
    import numpy as _np
    import concourse.bacc as _bacc
    from concourse import mybir as _mybir
    from concourse.bass_utils import run_bass_kernel_spmd as _run

    nc = _bacc.Bacc("TRN2", target_bir_lowering=False, num_devices=1)
    I = {name: _np.asarray(value) for name, value in inputs.items()}
    f4 = _np.float32

    def blocks(a, axis):
        a = _np.moveaxis(a, axis, -1)
        o = _np.zeros(a.shape[:-1] + (2, 4, 32), f4)
        o[..., :HD] = a.reshape(a.shape[:-1] + (2, 4, HD))
        return o.reshape(a.shape[:-1] + (2, P))

    n = _np.arange(NP, dtype=f4) / f4(NP - 1)
    t = _np.arange(P) % TOK
    grid = _np.stack([_np.tile(_np.repeat(n, NP), 2), _np.tile(_np.tile(n, NP), 2), _np.ones(P, f4)])
    r = _np.arange(P)
    row_pow = _np.zeros((P, 2), f4)
    row_pow[:64, 0] = f4(4) ** _np.arange(64)
    row_pow[64:, 1] = f4(4) ** _np.arange(64)
    ones_at = _np.zeros((P, 2), f4)
    ones_at[HD::32] = SC0_INV
    bq = blocks(I["L1_attn_bq"], 0).T.copy()
    bq[HD::32] = ones_at[HD::32]
    e8 = _np.arange(EXPERTS)
    sel3 = _np.zeros((3 * EXPERTS, EXPERTS, D), f4)
    sel3[_np.arange(3 * EXPERTS), _np.tile(e8, 3)] = 1
    wo = I["L0_attn_Wo"].reshape(D, TOK, 2, 2, 2)
    fields = {
        "Wp": I["L0_tok_Wp"].reshape(KX, P, D).transpose(1, 0, 2),
        "posW2": _np.concatenate([I["L0_tok_W2"], I["L0_tok_b2"][None], I["L0_tok_bp"][None]]),
        "posW1": _np.concatenate([I["L0_tok_W1"], I["L0_tok_b1"][None]]),
        "grid": grid,
        "ident": _np.eye(P, dtype=f4),
        "Wq0": I["L0_attn_Wq"].reshape(4, P, D).transpose(1, 0, 2),
        "Wk0": _np.concatenate([I["L0_attn_Wk"]] * 2),
        "WvT": _np.concatenate([I["L0_attn_Wv"].T] * 2, axis=1),
        "WoT": wo.transpose(3, 1, 4, 2, 0),
        "col_idx": r.astype(f4)[:, None],
        "row_pow": row_pow,
        "w1f": I["L0_ffn_w1"],
        "w2f": I["L0_ffn_w2"].reshape(HID // P, P, D).transpose(1, 0, 2),
        "b2f": I["L0_ffn_b2"],
        "ones_row": _np.ones((1, P), f4),
        "wr": I["L0_ffn_wr"],
        "br": _np.broadcast_to(I["L0_ffn_br"], (P, 1)),
        "b1f": I["L0_ffn_b1"].reshape(HID // P, P).T,
        "eye2": (t[:, None] == _np.arange(TOK)).astype(f4),
        "earlier": (_np.arange(TOK) < t[:, None]).astype(f4),
        "Wq1": blocks(I["L1_attn_Wq"], 1),
        "Wk1": blocks(I["L1_attn_Wk"], 1),
        "Wv1": I["L1_attn_Wv"],
        "Wo1": I["L1_attn_Wo"],
        "bv_rep": _np.broadcast_to(I["L1_attn_bv"], (P, D)),
        "bo_rep": _np.broadcast_to(I["L1_attn_bo"], (P, D)),
        "We": _np.concatenate([I["L1_attn_We"], I["L1_attn_be"][None]]),
        "bq1": bq,
        "bk1": blocks(I["L1_attn_bk"], 0).T,
        "rwT": I["L1_ffn_router_w"].T,
        "w1e": I["L1_ffn_w1"].transpose(1, 0, 2),
        "w2e": I["L1_ffn_w2"].reshape(EXPERTS // 2, P, D).transpose(1, 0, 2),
        "b2e": I["L1_ffn_b2"],
        "b1e": I["L1_ffn_b1"].reshape(EXPERTS // 2, P).T,
        "earlier8": _np.broadcast_to((e8 < e8[:, None]).astype(f4).reshape(-1), (P, EXPERTS * EXPERTS)),
        "sel3": sel3,
    }
    arrays = {}
    for group, parts in FIELDS.items():
        packed = _np.zeros((P, width(group)), f4)
        o = 0
        for name, rows, cols in parts:
            packed[:rows, o:o + cols] = fields[name].reshape(rows, cols)
            o += cols
        arrays[group] = packed
    x = I["x"].reshape(2, 4, CH, NP, PATCH, NP, PATCH)
    x = x.transpose(2, 4, 6, 0, 1, 3, 5).reshape(KX, P, 2, 4 * TOK)
    arrays["x"] = _np.ascontiguousarray(x.transpose(1, 2, 0, 3))
    packs = {}
    for name in list(arrays):
        a = arrays.pop(name)
        arrays[f"in_{name}_dram"] = a
        packs[name] = nc.dram_tensor(f"in_{name}_dram", a.shape, _mybir.dt.from_np(a.dtype), kind="ExternalInput").ap()
    args = {}
    for name in ("L1_attn_edge_index", "L1_attn_edge_attr"):
        a = _np.ascontiguousarray(I[name])
        arrays[f"in_{name}_dram"] = a
        args[name] = nc.dram_tensor(f"in_{name}_dram", a.shape, _mybir.dt.from_np(a.dtype), kind="ExternalInput").ap()
    outs = []
    for i, (shape, dtype) in enumerate(_OUTS):
        dt = _mybir.dt.from_np(_np.dtype(dtype))
        outs.append(nc.dram_tensor(f"out_{i}_dram", shape, dt, kind="ExternalOutput").ap())
    vit_tower(nc, args, packs, outs[0])
    r = _run(nc, [arrays], core_ids=[0])
    return r.results[0]["out_0_dram"]
```
